# Optimizing a Trainium2 kernel written in Bass

```python
import numpy as np
import jax
import jax.numpy as jnp

def _softmax(x, axis=-1):
    return jax.nn.softmax(x, axis=axis)

def _gelu(x):
    return jax.nn.gelu(x, approximate=True)

def _silu(x):
    return jax.nn.silu(x)

def _sigmoid(x):
    return jax.nn.sigmoid(x)

def _layernorm(x, axis=-1, eps=1e-05):
    m = jnp.mean(x, axis=axis, keepdims=True)
    v = jnp.var(x, axis=axis, keepdims=True)
    return (x - m) / jnp.sqrt(v + eps)

def _scatter_add(tgt, idx, src, axis=0):
    return tgt.at[idx].add(src)

def _segment_sum(src, seg, n):
    return jax.ops.segment_sum(src, seg, n)
kernel_name = 'mk_adj_resnorm_d1_adj_r2_861b0e'

def setup_inputs(seed: int=0):
    np.random.seed(seed)
    _w = jnp.asarray

    def _rec_inputs():
        import jax
        import jax.numpy as jnp
        _gk = jax.random.key(seed)
        x = 7.22e-05 + 1 * jax.random.normal(jax.random.fold_in(_gk, 1), (64, 128, 256), jnp.float32)
        _a = jax.random.bernoulli(jax.random.fold_in(_gk, 2), 0.0625, (64, 128, 128))
        _a = jnp.logical_or(_a, jnp.swapaxes(_a, -1, -2))
        _a = jnp.logical_or(_a, jnp.eye(128, dtype=bool))
        _af = _a.astype(jnp.float32)
        _af = _af * jax.random.uniform(jax.random.fold_in(_gk, 3), (64, 128, 128), jnp.float32, 0.05, 1)
        adj = _af
        return (x, adj)
    x, adj = _rec_inputs()

    def _L0_gnn_setup():
        import jax, jax.numpy as jnp
        import numpy as np
        EPS_LN = 1e-05

        def hypergraph_conv(x, adj, W, b):
            N, C, _ = adj.shape
            H = (adj != 0).astype(x.dtype)
            w = adj.reshape(N, -1)[:, :C]
            xw = jnp.einsum('ncd,hd->nch', x, W)
            Dn = jnp.einsum('nce,ne->nc', H, w)
            Dn = jnp.where(Dn > 0, 1.0 / Dn, 0.0)
            Be = H.sum(axis=1)
            Be = jnp.where(Be > 0, 1.0 / Be, 0.0)
            m = Be[:, :, None] * jnp.einsum('nce,nch->neh', H, xw)
            out = Dn[:, :, None] * jnp.einsum('nce,neh->nch', H, m)
            return out + b

        def layer_norm(x, g, b):
            mu = jnp.mean(x, axis=-1, keepdims=True)
            var = jnp.var(x, axis=-1, keepdims=True)
            return (x - mu) * jax.lax.rsqrt(var + EPS_LN) * g + b
        key = jax.random.key(seed)
        ks = jax.random.split(key, 4)
        N, C, Din, Dh, Dout = (16, 512, 256, 512, 256)
        x = jax.random.normal(ks[0], (N, C, Din), dtype=jnp.float32)
        adj = jax.random.uniform(ks[1], (N, C, C), dtype=jnp.float32, minval=0.1, maxval=1.0)
        W1 = jax.random.normal(ks[2], (Dh, Din), dtype=jnp.float32) * (1.0 / np.sqrt(Din))
        b1 = jnp.zeros((Dh,), dtype=jnp.float32)
        gamma = jnp.ones((Dh,), dtype=jnp.float32)
        beta = jnp.zeros((Dh,), dtype=jnp.float32)
        W2 = jax.random.normal(ks[3], (Dout, Dh), dtype=jnp.float32) * (1.0 / np.sqrt(Dh))
        b2 = jnp.zeros((Dout,), dtype=jnp.float32)
        return {'x': x, 'adj': adj, 'W1': W1, 'b1': b1, 'gamma': gamma, 'beta': beta, 'W2': W2, 'b2': b2}
    _L0_gnn_all = _L0_gnn_setup()
    _L0_gnn_in = {k: v for k, v in _L0_gnn_all.items() if k in ('W1', 'b1', 'gamma', 'beta', 'W2', 'b2')}
    del _L0_gnn_all
    return {'x': x, 'adj': adj, 'L0_gnn_W1': _L0_gnn_in['W1'], 'L0_gnn_b1': _L0_gnn_in['b1'], 'L0_gnn_gamma': _L0_gnn_in['gamma'], 'L0_gnn_beta': _L0_gnn_in['beta'], 'L0_gnn_W2': _L0_gnn_in['W2'], 'L0_gnn_b2': _L0_gnn_in['b2']}

def reference(x, adj, L0_gnn_W1, L0_gnn_b1, L0_gnn_gamma, L0_gnn_beta, L0_gnn_W2, L0_gnn_b2):
    import jax
    import jax.numpy as jnp

    def _L0_gnn_ref(x, adj, W1, b1, gamma, beta, W2, b2):
        import jax, jax.numpy as jnp
        import numpy as np
        EPS_LN = 1e-05

        def hypergraph_conv(x, adj, W, b):
            N, C, _ = adj.shape
            H = (adj != 0).astype(x.dtype)
            w = adj.reshape(N, -1)[:, :C]
            xw = jnp.einsum('ncd,hd->nch', x, W)
            Dn = jnp.einsum('nce,ne->nc', H, w)
            Dn = jnp.where(Dn > 0, 1.0 / Dn, 0.0)
            Be = H.sum(axis=1)
            Be = jnp.where(Be > 0, 1.0 / Be, 0.0)
            m = Be[:, :, None] * jnp.einsum('nce,nch->neh', H, xw)
            out = Dn[:, :, None] * jnp.einsum('nce,neh->nch', H, m)
            return out + b

        def layer_norm(x, g, b):
            mu = jnp.mean(x, axis=-1, keepdims=True)
            var = jnp.var(x, axis=-1, keepdims=True)
            return (x - mu) * jax.lax.rsqrt(var + EPS_LN) * g + b
        h = jax.nn.relu(hypergraph_conv(x, adj, W1, b1))
        h = layer_norm(h, gamma, beta)
        y = hypergraph_conv(h, adj, W2, b2)
        return y + x
    x = _layernorm(x + _L0_gnn_ref(x, adj, L0_gnn_W1, L0_gnn_b1, L0_gnn_gamma, L0_gnn_beta, L0_gnn_W2, L0_gnn_b2), axis=-1)
    return x

_drawn_inputs = setup_inputs


def setup_inputs(seed=0):
    import zlib

    import numpy as np

    out = dict(_drawn_inputs(seed))
    spreads = {'L0_gnn_b1': (0.0, 0.1),
     'L0_gnn_gamma': (1.0, 0.2),
     'L0_gnn_beta': (0.0, 0.1),
     'L0_gnn_b2': (0.0, 0.342)}
    factors = {}
    for name, (base, spread) in spreads.items():
        noise = np.random.default_rng([zlib.crc32(name.encode()), seed]).standard_normal(out[name].shape)
        drawn = base * np.exp(spread * noise) if base else spread * noise
        out[name] = jnp.asarray(drawn.astype(out[name].dtype))
    for name, factor in factors.items():
        out[name] = (out[name] * factor).astype(out[name].dtype)
    return out
```

```python
from contextlib import ExitStack

import concourse.bass as bass
from concourse import mybir

ALU = mybir.AluOpType
ACT = mybir.ActivationFunctionType
AX = mybir.AxisListType
F32 = mybir.dt.float32
F32R = mybir.dt.float32r
BF16 = mybir.dt.bfloat16

P = 128
PER = 4
BANK = 512
EPS = 1e-5
TINY = 1e-30


def hypergraph_block(nc, x, adj, W1, b1, gamma, beta, W2, b2, out):
    N, C, DIN = x.shape
    HID = W1.shape[0]
    DOUT = W2.shape[0]
    KD, KH = DIN // P, HID // P
    GROUPS = N // PER
    assert C == P and DIN == DOUT == 2 * P and HID == BANK and GROUPS % 2 == 0
    W2COLS = DOUT + 2

    x_dram = x.rearrange("n c d -> c n d")
    adj_dram = adj.rearrange("n c e -> c n e")
    out_dram = out.rearrange("n c d -> c n d")

    with ExitStack() as ctx:
        def sb(name, shape, dt=F32):
            return ctx.enter_context(nc.sbuf_tensor(name, shape, dt))

        def sem(name):
            return ctx.enter_context(nc.semaphore(name))

        ident = sb("ident", [P, P])
        ident_b = sb("ident_b", [P, P], BF16)
        ones = sb("ones", [P, P])
        half_power = sb("half_power", [P, PER])
        w1_raw = sb("w1_raw", [P, KH, DIN])
        w2_raw = sb("w2_raw", [P, KD, HID])
        vec_rows = sb("vec_rows", [3 * KH, P])
        vec = sb("vec", [P, 3 * KH])
        w1_hi = sb("w1_hi", [P, KD, HID], F32R)
        w1_lo = sb("w1_lo", [P, KD, HID], F32R)
        w2_t = sb("w2_t", [P, KH, DOUT])
        w2_g = sb("w2_g", [P, KH, DOUT])
        w2_mean = sb("w2_mean", [P, DOUT])
        beta_b = sb("beta_b", [P, KH, P])
        w2_hi = sb("w2_hi", [P, KH, W2COLS], F32R)
        w2_lo = sb("w2_lo", [P, KH, DOUT], F32R)
        c2 = sb("c2", [P, DOUT])
        b2_half = sb("b2_half", [P, DOUT])

        adj_sb = sb("adj_sb", [P, 2, PER, P])
        w_sb = sb("w_sb", [P, 2, PER, P])
        x_sb = sb("x_sb", [P, 2, PER, DIN])
        xb_sb = sb("xb_sb", [P, 2, PER, DIN])
        h_sb = sb("h_sb", [P, PER, P], BF16)
        hw_sb = sb("hw_sb", [P, PER, P])
        degree = sb("degree", [P, 4, PER])
        hd_sb = sb("hd_sb", [P, PER, P])
        ht_sb = sb("ht_sb", [P, PER, P])
        members = sb("members", [P, PER])
        binv = sb("binv", [P, 2, PER])
        htdb_sb = sb("htdb_sb", [P, PER, P])
        at_sb = sb("at_sb", [P, 2, PER, P])
        u_hi = sb("u_hi", [P, KD, PER * P], F32R)
        u_lo = sb("u_lo", [P, KD, PER * P], F32R)
        r_sb = sb("r_sb", [P, KH, PER * P])
        r_hi = sb("r_hi", [P, KH, PER * P], F32R)
        r_lo = sb("r_lo", [P, KH, PER * P], F32R)
        sq_sb = sb("sq_sb", [P, KH, PER * P])
        pair_sb = sb("pair_sb", [P, 2, PER * P])
        q_sb = sb("q_sb", [P, PER * P])
        stat1 = sb("stat1", [P, 4, PER])
        rstd1 = sb("rstd1", [P, PER])
        g_sb = sb("g_sb", [P, PER, DOUT])
        z_sb = sb("z_sb", [P, 2, PER, DOUT])
        bn_sb = sb("bn_sb", [P, PER, 6])
        mv_sb = sb("mv_sb", [P, PER, 2])
        var2 = sb("var2", [P, PER])
        rstd2 = sb("rstd2", [P, PER])

        bank_h = ctx.enter_context(nc.psum_tensor("bank_h", [P, BANK], F32))
        bank_hd = ctx.enter_context(nc.psum_tensor("bank_hd", [P, BANK], F32))
        bank_v = ctx.enter_context(nc.psum_tensor("bank_v", [P, 2, BANK], F32))
        bank_g = ctx.enter_context(nc.psum_tensor("bank_g", [P, PER, BANK], F32))
        bank_h_bf = bank_h[:, :].bitcast(BF16)
        SUM, SQ = DOUT, 3 * P

        weights_in = [sem(f"weights_in{n}") for n in range(4)]
        adj_in = [sem("adj_in_even"), sem("adj_in_odd")]
        x_in = [sem("x_in_even"), sem("x_in_odd")]
        stored = [sem("stored_even"), sem("stored_odd")]
        consts_zeroed = sem("consts_zeroed")
        consts_ready = sem("consts_ready")
        vec_turned, vec_ready = sem("vec_turned"), sem("vec_ready")
        w1_turned, w1_step, w1_ready = sem("w1_turned"), sem("w1_step"), sem("w1_ready")
        w2_turned, w2_step, w2_scaled = sem("w2_turned"), sem("w2_step"), sem("w2_scaled")
        w2_summed, w2_ready = sem("w2_summed"), sem("w2_ready")
        degree_step, d_ready = sem("degree_step"), sem("d_ready")
        hd_ready, h_turned, hd_turned = sem("hd_ready"), sem("h_turned"), sem("hd_turned")
        ht_ready, b_step, b_ready, htdb_ready = sem("ht_ready"), sem("b_step"), sem("b_ready"), sem("htdb_ready")
        at_made, at_ready = sem("at_made"), sem("at_ready")
        u_made, u_hi_ready, u_lo_ready = sem("u_made"), sem("u_hi_ready"), sem("u_lo_ready")
        v_made, relu_ready, sq_ready = sem("v_made"), sem("relu_ready"), sem("sq_ready")
        r_hi_ready, r_lo_ready = sem("r_hi_ready"), sem("r_lo_ready")
        pairs_ready, q_ready = sem("pairs_ready"), sem("q_ready")
        g_made, stat1_step, var1_ready, rstd1_ready = sem("g_made"), sem("stat1_step"), sem("var1_ready"), sem("rstd1_ready")
        g_ready, y_made = sem("g_ready"), sem("y_made")
        xb_ready, z_ready, stat2_step = sem("xb_ready"), sem("z_ready"), sem("stat2_step")
        pool_passed = sem("pool_passed")
        var2_ready, rstd2_ready, out_ready = sem("var2_ready"), sem("rstd2_ready"), sem("out_ready")

        def graph(n):
            return slice(n * P, (n + 1) * P)

        def arrival(i, odd, times):
            return (i - odd) * (8 * times) + 16 * times

        def pipeline(eng, step):
            step(0, 0, first=True)
            step(1, 1)
            step(2, 0)
            with eng.Fori(0, GROUPS // 2 - 2) as t:
                step(t * 2 + 3, 1)
                step(t * 2 + 4, 0)
            step(GROUPS - 1, 1, last=True)

        block = ctx.enter_context(nc.Block())

        @block.sync
        def _(sp):
            def load_adj(i, odd):
                sp.dma_start(adj_sb[:, odd], adj_dram[:, bass.ds(i * PER, PER)]).then_inc(adj_in[odd], 16)
                row = adj[bass.ds(i * PER, PER), 0, :].unsqueeze(0).to_broadcast([P, PER, P])
                sp.dma_start(w_sb[:, odd], row).then_inc(adj_in[odd], 16)

            def load_x(i, odd):
                sp.dma_start(x_sb[:, odd], x_dram[:, bass.ds(i * PER, PER)]).then_inc(x_in[odd], 16)

            def load_ahead(i, odd):
                sp.wait_ge(d_ready, i + 1)
                load_adj(i + 2, odd)
                sp.wait_ge(u_made, (i + 1) * KD)
                sp.wait_ge(xb_ready, i + 1)
                load_x(i + 2, odd)

            def store(i, odd):
                sp.wait_ge(out_ready, i + 1)
                sp.dma_start(out_dram[:, bass.ds(i * PER, PER)], z_sb[:, odd]).then_inc(stored[odd], 16)

            load_adj(0, 0)
            sp.dma_start(vec_rows[0:KH, :], b1.rearrange("(k p) -> k p", p=P)).then_inc(weights_in[0], 16)
            sp.dma_start(vec_rows[KH:2 * KH, :], gamma.rearrange("(k p) -> k p", p=P)).then_inc(weights_in[0], 16)
            sp.dma_start(vec_rows[2 * KH:3 * KH, :], beta.rearrange("(k p) -> k p", p=P)).then_inc(weights_in[0], 16)
            sp.dma_start(w1_raw[:, :, :], W1.rearrange("(k p) d -> p k d", p=P)).then_inc(weights_in[1], 16)
            load_x(0, 0)
            sp.dma_start(w2_raw[:, :, :], W2.rearrange("(k p) h -> p k h", p=P)).then_inc(weights_in[2], 16)
            sp.dma_start(b2_half[:, :], b2.unsqueeze(0).to_broadcast([P, DOUT])).then_inc(weights_in[3], 16)
            load_adj(1, 1)
            load_x(1, 1)
            load_ahead(0, 0)
            with sp.Fori(0, GROUPS // 2 - 2) as t:
                load_ahead(t * 2 + 1, 1)
                store(t * 2, 0)
                load_ahead(t * 2 + 2, 0)
                store(t * 2 + 1, 1)
            load_ahead(GROUPS - 3, 1)
            for i in range(GROUPS - 4, GROUPS):
                store(i, i % 2)
            for odd in range(2):
                sp.wait_ge(stored[odd], 8 * GROUPS)

        @block.tensor
        def _(pe):
            def turn_h(j):
                pe.wait_ge(hd_ready, j + 1)
                pe.wait_ge(at_ready, j)
                for n in range(PER):
                    mm = pe.transpose(bank_h_bf[:, graph(n)], h_sb[:, n], ident_b[:, :])
                mm.then_inc(h_turned, 1)
                pe.wait_ge(htdb_ready, j)
                for n in range(PER):
                    mm = pe.transpose(bank_hd[:, graph(n)], hd_sb[:, n], ident[:, :])
                mm.then_inc(hd_turned, 1)

            def make_at(j):
                pe.wait_ge(ht_ready, j + 1)
                pe.wait_ge(htdb_ready, j + 1)
                for n in range(PER):
                    mm = pe.matmul(bank_h[:, graph(n)], ht_sb[:, n], htdb_sb[:, n], start=True, stop=True)
                mm.then_inc(at_made, 1)

            def make_u(j, odd, bank_free):
                pe.wait_ge(at_ready, j + 1)
                pe.wait_ge(x_in[odd], arrival(j, odd, 1))
                for c in range(KD):
                    bank_free(c)
                    for n in range(PER):
                        mm = pe.matmul(bank_v[:, c, graph(n)], x_sb[:, odd, n, graph(c)], at_sb[:, odd, n],
                                       start=True, stop=True)
                    mm.then_inc(u_made, 1)

            def make_v(i, k):
                if k < 2:
                    pe.wait_ge(u_lo_ready, (i + 1) * KD)
                else:
                    pe.wait_ge(relu_ready, i * KH + (k - 1))
                terms = [(w, u, c) for w, u in ((w1_hi, u_hi), (w1_lo, u_hi), (w1_hi, u_lo)) for c in range(KD)]
                for m, (w, u, c) in enumerate(terms):
                    mm = pe.matmul(bank_v[:, k % 2], w[:, c, graph(k)], u[:, c],
                                   start=(m == 0), stop=(m == len(terms) - 1))
                mm.then_inc(v_made, 1)

            def make_g(i, n):
                for k in range(KH):
                    pe.matmul(bank_g[:, n, 0:W2COLS], r_hi[:, k, graph(n)], w2_hi[:, k], start=(k == 0), stop=False)
                    pe.matmul(bank_g[:, n, 0:DOUT], r_hi[:, k, graph(n)], w2_lo[:, k], start=False, stop=False,
                              skip_group_check=True)
                    pe.matmul(bank_g[:, n, 0:W2COLS], r_lo[:, k, graph(n)], w2_hi[:, k], start=False,
                              stop=(k == KH - 1))
                mm = pe.matmul(bank_g[:, n, SQ:SQ + P], q_sb[:, graph(n)], ones[:, :], start=True, stop=True)
                if n == PER - 1:
                    mm.then_inc(g_made, 1)

            def make_y(i, odd):
                pe.wait_ge(g_ready, i + 1)
                for half in range(2):
                    pe.wait_ge(relu_ready, (i + 1) * KH + 3 + half)
                    for n in range(2 * half, 2 * half + 2):
                        mm = pe.matmul(bank_v[:, half, (n % 2) * DOUT:(n % 2 + 1) * DOUT], at_sb[:, odd, n],
                                       g_sb[:, n], start=True, stop=True)
                    mm.then_inc(y_made, 1)

            pe.wait_ge(consts_ready, 2)
            pe.wait_ge(weights_in[0], 48)
            pe.transpose(bank_v[:, 0, 0:3 * KH], vec_rows[:, :], ident[0:3 * KH, 0:3 * KH]).then_inc(vec_turned, 1)
            turn_h(0)
            pe.wait_ge(weights_in[1], 16)
            for c in range(KD):
                for k in range(KH):
                    mm = pe.transpose(bank_g[:, c, graph(k)], w1_raw[:, k, graph(c)], ident[:, :])
            mm.then_inc(w1_turned, 1)
            make_at(0)
            pe.wait_ge(weights_in[2], 16)
            for k in range(KH):
                for c in range(KD):
                    mm = pe.transpose(bank_g[:, 2 + k // 2, (k % 2) * DOUT + c * P:(k % 2) * DOUT + (c + 1) * P],
                                      w2_raw[:, c, graph(k)], ident[:, :])
            mm.then_inc(w2_turned, 1)
            make_u(0, 0, lambda c: pe.wait_ge(vec_ready, 1))

            def sum_w2():
                pe.wait_ge(w2_scaled, 1)
                pe.wait_ge(w1_ready, 1)
                for k in range(KH):
                    pe.matmul(bank_g[:, 0, 0:DOUT], ones[:, :], w2_g[:, k], start=(k == 0), stop=(k == KH - 1))
                for k in range(KH):
                    mm = pe.matmul(bank_g[:, 1, 0:DOUT], beta_b[:, k], w2_t[:, k], start=(k == 0), stop=(k == KH - 1))
                mm.then_inc(w2_summed, 1)

            def step(i, odd, first=False, last=False):
                if first:
                    pe.wait_ge(w1_ready, 1)
                for k in range(3):
                    make_v(i, k)
                if not last:
                    turn_h(i + 1)
                make_v(i, 3)
                if first:
                    sum_w2()
                else:
                    make_y(i - 1, 1 - odd)
                if not last:
                    make_at(i + 1)
                pe.wait_ge(r_hi_ready, (i + 1) * KH)
                pe.wait_ge(r_lo_ready, (i + 1) * KH)
                pe.wait_ge(q_ready, i + 1)
                if first:
                    pe.wait_ge(w2_ready, 1)
                make_g(i, 0)
                if not last:
                    if first:
                        make_u(i + 1, 1 - odd, lambda c: pe.wait_ge(relu_ready, KH - 1 + c))
                    else:
                        make_u(i + 1, 1 - odd, lambda c: pe.wait_ge(z_ready, i * 2 - 1 + c))
                for n in range(1, PER):
                    make_g(i, n)

            pipeline(pe, step)
            make_y_last = GROUPS - 1
            pe.wait_ge(g_ready, GROUPS)
            for half in range(2):
                for n in range(2 * half, 2 * half + 2):
                    mm = pe.matmul(bank_v[:, half, (n % 2) * DOUT:(n % 2 + 1) * DOUT], at_sb[:, make_y_last % 2, n],
                                   g_sb[:, n], start=True, stop=True)
                mm.then_inc(y_made, 1)

        @block.scalar
        def _(act):
            def make_hd(j):
                act.wait_ge(d_ready, j + 1)
                act.wait_ge(hd_turned, j)
                for n in range(PER):
                    ins = nc.scalar.activation(hd_sb[:, n], h_sb[:, n], ACT.Copy, scale=degree[:, 3, n:n + 1])
                ins.then_inc(hd_ready, 1)

            def read_ht(j):
                act.wait_ge(h_turned, j + 1)
                act.wait_ge(at_made, j)
                act.wait_ge(b_ready, j)
                for n in range(PER):
                    ins = nc.scalar.activation(ht_sb[:, n], bank_h_bf[:, graph(n)], ACT.Copy,
                                               accum_out=members[:, n:n + 1])
                ins.then_inc(ht_ready, 1)

            def read_htdb(j):
                act.wait_ge(hd_turned, j + 1)
                act.wait_ge(b_ready, j + 1)
                for n in range(PER):
                    ins = nc.scalar.activation(htdb_sb[:, n], bank_hd[:, graph(n)], ACT.Copy,
                                               scale=binv[:, 1, n:n + 1])
                ins.then_inc(htdb_ready, 1)

            def read_at(j, odd):
                act.wait_ge(at_made, j + 1)
                nc.scalar.activation(at_sb[:, odd].rearrange("p n c -> p (n c)"), bank_h[:, :],
                                     ACT.Copy).then_inc(at_ready, 1)

            def split_u(j):
                for c in range(KD):
                    act.wait_ge(u_made, j * KD + (c + 1))
                    nc.scalar.activation(u_hi[:, c], bank_v[:, c], ACT.Copy).then_inc(u_hi_ready, 1)

            def relu(i, k, first):
                act.wait_ge(v_made, i * KH + (k + 1))
                if not first:
                    act.wait_ge(r_lo_ready, i * KH + (k + 1 - KH))
                nc.scalar.activation(r_sb[:, k], bank_v[:, k % 2], ACT.Relu,
                                     bias=vec[:, k:k + 1]).then_inc(relu_ready, 1)

            def square(i, k, first):
                act.wait_ge(relu_ready, i * KH + (k + 1))
                if not first:
                    act.wait_ge(pairs_ready, i * 2 + (k // 2 - 1))
                nc.scalar.activation(sq_sb[:, k], r_sb[:, k], ACT.Square).then_inc(sq_ready, 1)

            act.wait_ge(vec_turned, 1)
            nc.scalar.activation(vec[:, :], bank_v[:, 0, 0:3 * KH], ACT.Copy).then_inc(vec_ready, 1)
            make_hd(0)
            read_ht(0)
            read_htdb(0)
            read_at(0, 0)
            split_u(0)
            act.wait_ge(vec_ready, 1)

            def step(i, odd, first=False, last=False):
                if not last:
                    make_hd(i + 1)
                for k in range(3):
                    relu(i, k, first)
                    square(i, k, first)
                if not last:
                    read_ht(i + 1)
                relu(i, 3, first)
                if not last:
                    read_htdb(i + 1)
                square(i, 3, first)
                if not last:
                    read_at(i + 1, 1 - odd)
                    split_u(i + 1)

            pipeline(act, step)

        @block.vector
        def _(dve):
            def make_d(j, odd):
                dve.wait_ge(adj_in[odd], arrival(j, odd, 2))
                dve.wait_ge(h_turned, j)
                nc.vector.tensor_scalar(h_sb[:, :, :], adj_sb[:, odd], 0.0, None, ALU.not_equal)
                for n in range(PER):
                    ins = nc.vector.scalar_tensor_tensor(out=hw_sb[:, n], in0=adj_sb[:, odd, n], scalar=0.0,
                                                         in1=w_sb[:, odd, n], op0=ALU.not_equal, op1=ALU.mult,
                                                         accum_out=degree[:, 0, n:n + 1])
                ins.then_inc(degree_step, 1)
                dve.wait_ge(degree_step, j * 3 + 1)
                nc.vector.tensor_scalar(degree[:, 1], degree[:, 0], TINY, None, ALU.max).then_inc(degree_step, 1)
                dve.wait_ge(degree_step, j * 3 + 2)
                nc.vector.reciprocal(degree[:, 2], degree[:, 1]).then_inc(degree_step, 1)
                dve.wait_ge(degree_step, j * 3 + 3)
                dve.wait_ge(hd_ready, j)
                nc.vector.scalar_tensor_tensor(out=degree[:, 3], in0=degree[:, 0], scalar=0.0, in1=degree[:, 2],
                                               op0=ALU.is_gt, op1=ALU.mult).then_inc(d_ready, 1)

            def make_b(j):
                dve.wait_ge(ht_ready, j + 1)
                nc.vector.tensor_scalar(binv[:, 0], members[:, :], 1.0, None, ALU.max).then_inc(b_step, 1)
                dve.wait_ge(b_step, j + 1)
                dve.wait_ge(htdb_ready, j)
                nc.vector.reciprocal(binv[:, 1], binv[:, 0]).then_inc(b_ready, 1)

            def split_u(j, chunks=range(KD)):
                for c in chunks:
                    dve.wait_ge(u_hi_ready, j * KD + (c + 1))
                    nc.vector.tensor_tensor(u_lo[:, c], bank_v[:, c], u_hi[:, c].bitcast(F32),
                                            ALU.subtract).then_inc(u_lo_ready, 1)

            def make_var1(i):
                dve.wait_ge(g_made, i + 1)
                nc.vector.tensor_scalar(stat1[:, 0], bank_g[:, :, SUM], 1.0 / HID, None,
                                        ALU.mult).then_inc(stat1_step, 1)
                dve.wait_ge(stat1_step, i * 3 + 1)
                nc.vector.tensor_tensor(stat1[:, 1], stat1[:, 0], stat1[:, 0], ALU.mult).then_inc(stat1_step, 1)
                dve.wait_ge(stat1_step, i * 3 + 2)
                nc.vector.scalar_tensor_tensor(out=stat1[:, 2], in0=bank_g[:, :, SQ], scalar=1.0 / HID,
                                               in1=stat1[:, 1], op0=ALU.mult,
                                               op1=ALU.subtract).then_inc(stat1_step, 1)
                dve.wait_ge(stat1_step, i * 3 + 3)
                nc.vector.tensor_scalar(stat1[:, 3], stat1[:, 2], 0.0, EPS, ALU.max,
                                        ALU.add).then_inc(var1_ready, 1)

            def read_g(i, first):
                dve.wait_ge(rstd1_ready, i + 1)
                if not first:
                    dve.wait_ge(y_made, i * 2)
                for n in range(PER):
                    ins = nc.vector.scalar_tensor_tensor(out=g_sb[:, n], in0=bank_g[:, n, 0:DOUT],
                                                         scalar=rstd1[:, n:n + 1], in1=c2[:, :],
                                                         op0=ALU.mult, op1=ALU.add)
                ins.then_inc(g_ready, 1)

            def split_r(i, k):
                dve.wait_ge(r_hi_ready, i * KH + (k + 1))
                nc.vector.tensor_tensor(r_lo[:, k], r_sb[:, k], r_hi[:, k].bitcast(F32),
                                        ALU.subtract).then_inc(r_lo_ready, 1)

            def sum_pair(i, pair):
                dve.wait_ge(sq_ready, i * KH + (2 * pair + 2))
                nc.vector.tensor_tensor(pair_sb[:, pair], sq_sb[:, 2 * pair], sq_sb[:, 2 * pair + 1],
                                        ALU.add).then_inc(pairs_ready, 1)

            def finish_z(i, odd, stored_before, between=None):
                if stored_before is not None:
                    dve.wait_ge(stored[odd], stored_before)
                dve.wait_ge(xb_ready, i + 1)
                for half in range(2):
                    dve.wait_ge(y_made, i * 2 + (half + 1))
                    pair = slice(2 * half, 2 * half + 2)
                    nc.vector.scalar_tensor_tensor(out=z_sb[:, odd, pair].rearrange("p n d -> p (n d)"),
                                                   in0=xb_sb[:, odd, pair].rearrange("p n d -> p (n d)"),
                                                   scalar=2.0, in1=bank_v[:, half], op0=ALU.mult,
                                                   op1=ALU.add).then_inc(z_ready, 1)
                dve.wait_ge(z_ready, (i + 1) * 2)
                dve.wait_ge(out_ready, i)
                for n in range(PER):
                    ins = nc.vector.bn_stats(bn_sb[:, n], z_sb[:, odd, n])
                ins.then_inc(stat2_step, 1)
                dve.wait_ge(stat2_step, i * 2 + 1)
                if between:
                    between()
                for n in range(PER):
                    ins = nc.vector.bn_aggr(mv_sb[:, n], bn_sb[:, n])
                ins.then_inc(stat2_step, 1)
                dve.wait_ge(stat2_step, i * 2 + 2)
                nc.vector.tensor_scalar(var2[:, :], mv_sb[:, :, 1], EPS, None, ALU.add).then_inc(var2_ready, 1)

            make_d(0, 0)
            dve.wait_ge(w1_turned, 1)
            for c in range(KD):
                ins = nc.vector.tensor_copy(w1_hi[:, c], bank_g[:, c])
            ins.then_inc(w1_step, 1)
            make_b(0)
            dve.wait_ge(w1_step, 1)
            for c in range(KD):
                ins = nc.vector.tensor_tensor(w1_lo[:, c], bank_g[:, c], w1_hi[:, c].bitcast(F32), ALU.subtract)
            ins.then_inc(w1_ready, 1)
            split_u(0)

            def scale_w2():
                dve.wait_ge(w2_turned, 1)
                dve.wait_ge(vec_ready, 1)
                dve.wait_ge(consts_ready, 3)
                for k in range(KH):
                    turned = bank_g[:, 2 + k // 2, (k % 2) * DOUT:(k % 2 + 1) * DOUT]
                    nc.vector.tensor_copy(w2_t[:, k], turned)
                    nc.vector.tensor_scalar(w2_g[:, k], turned, vec[:, KH + k:KH + k + 1], None, ALU.mult)
                    ins = nc.vector.tensor_scalar(beta_b[:, k], ones[:, :], vec[:, 2 * KH + k:2 * KH + k + 1],
                                                  None, ALU.mult)
                ins.then_inc(w2_scaled, 1)

            def centre_w2():
                dve.wait_ge(w2_summed, 1)
                nc.vector.tensor_copy(c2[:, :], bank_g[:, 1, 0:DOUT])
                nc.vector.tensor_scalar(w2_mean[:, :], bank_g[:, 0, 0:DOUT], 1.0 / HID, None,
                                        ALU.mult).then_inc(w2_step, 1)
                dve.wait_ge(w2_step, 1)
                for k in range(KH):
                    ins = nc.vector.tensor_tensor(w2_g[:, k], w2_g[:, k], w2_mean[:, :], ALU.subtract)
                ins.then_inc(w2_step, 1)
                dve.wait_ge(w2_step, 2)
                for k in range(KH):
                    ins = nc.vector.tensor_copy(w2_hi[:, k, 0:DOUT], w2_g[:, k])
                ins.then_inc(w2_step, 1)
                dve.wait_ge(w2_step, 3)
                for k in range(KH):
                    ins = nc.vector.tensor_tensor(w2_lo[:, k], w2_g[:, k], w2_hi[:, k, 0:DOUT].bitcast(F32),
                                                  ALU.subtract)
                ins.then_inc(w2_ready, 1)

            def step(i, odd, first=False, last=False):
                if first:
                    scale_w2()
                else:
                    make_var1(i - 1)
                if not last:
                    make_d(i + 1, 1 - odd)
                if not first:
                    read_g(i - 1, first=False)
                split_r(i, 0)
                split_r(i, 1)
                sum_pair(i, 0)
                split_r(i, 2)
                if not last:
                    make_b(i + 1)
                split_r(i, 3)
                sum_pair(i, 1)
                dve.wait_ge(pairs_ready, i * 2 + 2)
                nc.vector.tensor_tensor(q_sb[:, :], pair_sb[:, 0], pair_sb[:, 1], ALU.add).then_inc(q_ready, 1)
                if first:
                    centre_w2()
                    split_u(i + 1)
                elif last:
                    finish_z(i - 1, 1 - odd, (i - 2 + odd) * 8)
                else:
                    finish_z(i - 1, 1 - odd, (i - 2 + odd) * 8, between=lambda: split_u(i + 1, [0]))
                    split_u(i + 1, [1])

            pipeline(dve, step)
            make_var1(GROUPS - 1)
            read_g(GROUPS - 1, first=False)
            finish_z(GROUPS - 1, 1, (GROUPS // 2 - 1) * 16)

        @block.gpsimd
        def _(pool):
            nc.gpsimd.memset(ident[:, :], 0.0).then_inc(consts_zeroed, 1)
            nc.gpsimd.memset(ident_b[:, :], 0.0).then_inc(consts_zeroed, 1)
            for n, m in enumerate((ident, ident_b)):
                pool.wait_ge(consts_zeroed, n + 1)
                nc.gpsimd.affine_select(out=m[:, :], in_=m[:, :], compare_op=ALU.not_equal, fill=1.0, base=0,
                                        pattern=[[-1, P]], channel_multiplier=1).then_inc(consts_ready, 1)
            nc.gpsimd.memset(half_power[:, :], -0.5)
            nc.gpsimd.memset(w2_hi[:, :, DOUT:W2COLS].bitcast(F32), 1.0)
            nc.gpsimd.memset(ones[:, :], 1.0).then_inc(consts_ready, 1)
            pool.wait_ge(consts_ready, 3)
            pool.wait_ge(weights_in[3], 16)
            nc.gpsimd.tensor_scalar(b2_half[:, :], b2_half[:, :], 0.5, 1.0, ALU.mult,
                                    ALU.mult).then_inc(consts_ready, 1)
            pool.wait_ge(consts_ready, 4)

            def inverse_std1(i):
                pool.wait_ge(var1_ready, i + 1)
                nc.gpsimd.tensor_tensor(rstd1[:, :], stat1[:, 3], half_power[:, :], ALU.pow).then_inc(rstd1_ready, 1)

            def add_b2(i, odd, y_before):
                pool.wait_ge(x_in[odd], arrival(i, odd, 1))
                if y_before is not None:
                    pool.wait_ge(z_ready, y_before)
                nc.gpsimd.tensor_tensor(xb_sb[:, odd], x_sb[:, odd],
                                        b2_half[:, :].unsqueeze(1).to_broadcast([P, PER, DOUT]),
                                        ALU.add).then_inc(xb_ready, 1)

            def split_r(i, k):
                pool.wait_ge(relu_ready, i * KH + (k + 1))
                pool.sem_inc(pool_passed, 1)
                nc.gpsimd.tensor_scalar(r_hi[:, k], r_sb[:, k], 1.0, 1.0, ALU.mult, ALU.mult).then_inc(r_hi_ready, 1)

            def normalise(i, odd):
                pool.wait_ge(var2_ready, i + 1)
                nc.gpsimd.tensor_tensor(rstd2[:, :], var2[:, :], half_power[:, :], ALU.pow).then_inc(rstd2_ready, 1)
                pool.wait_ge(rstd2_ready, i + 1)
                pool.sem_inc(pool_passed, 1)
                for n in range(PER):
                    ins = nc.gpsimd.tensor_scalar(z_sb[:, odd, n], z_sb[:, odd, n], mv_sb[:, n, 0:1],
                                                  rstd2[:, n:n + 1], ALU.subtract, ALU.mult)
                ins.then_inc(out_ready, 1)

            def step(i, odd, first=False, last=False):
                if not first:
                    inverse_std1(i - 1)
                for k in range(KH):
                    split_r(i, k)
                add_b2(i, odd, None if first else i * 2 - 2)
                if not first:
                    normalise(i - 1, 1 - odd)

            pipeline(pool, step)
            inverse_std1(GROUPS - 1)
            normalise(GROUPS - 1, 1)


_INS = ["x", "adj", "L0_gnn_W1", "L0_gnn_b1", "L0_gnn_gamma", "L0_gnn_beta", "L0_gnn_W2", "L0_gnn_b2"]


def kernel(**inputs):
    import numpy as _np
    import concourse.bacc as _bacc
    from concourse import mybir as _mybir
    from concourse.bass_utils import run_bass_kernel_spmd as _run

    nc = _bacc.Bacc("TRN2", target_bir_lowering=False, num_devices=1)
    arrays, args = {}, []
    for name in _INS:
        a = _np.ascontiguousarray(inputs[name])
        arrays[f"in_{name}_dram"] = a
        args.append(nc.dram_tensor(f"in_{name}_dram", a.shape, _mybir.dt.from_np(a.dtype), kind="ExternalInput").ap())
    args.append(nc.dram_tensor("out_dram", inputs["x"].shape, _mybir.dt.float32, kind="ExternalOutput").ap())
    hypergraph_block(nc, *args)
    r = _run(nc, [arrays], core_ids=[0])
    return r.results[0]["out_dram"]
```

```python
from contextlib import ExitStack

import concourse.bass as bass
from concourse import mybir

ALU = mybir.AluOpType
ACT = mybir.ActivationFunctionType
AX = mybir.AxisListType
F32 = mybir.dt.float32
F32R = mybir.dt.float32r
BF16 = mybir.dt.bfloat16

P = 128
PER = 4
BANK = 512
EPS = 1e-5
TINY = 1e-30


def hypergraph_block(nc, x, adj, W1, b1, gamma, beta, W2, b2, out):
    N, C, DIN = x.shape
    HID = W1.shape[0]
    DOUT = W2.shape[0]
    KD, KH = DIN // P, HID // P
    GROUPS = N // PER
    assert C == P and DIN == DOUT == 2 * P and HID == BANK and GROUPS % 2 == 0
    W2COLS = DOUT + 2

    x_dram = x.rearrange("n c d -> c n d")
    adj_dram = adj.rearrange("n c e -> c n e")
    out_dram = out.rearrange("n c d -> c n d")

    with ExitStack() as ctx:
        def sb(name, shape, dt=F32):
            return ctx.enter_context(nc.sbuf_tensor(name, shape, dt))

        def sem(name):
            return ctx.enter_context(nc.semaphore(name))

        ident = sb("ident", [P, P])
        ident_b = sb("ident_b", [P, P], BF16)
        ones = sb("ones", [P, P])
        half_power = sb("half_power", [P, PER])
        w1_raw = sb("w1_raw", [P, KH, DIN])
        w2_raw = sb("w2_raw", [P, KD, HID])
        vec_rows = sb("vec_rows", [3 * KH, P])
        vec = sb("vec", [P, 3 * KH])
        w1_hi = sb("w1_hi", [P, KD, HID], F32R)
        w1_lo = sb("w1_lo", [P, KD, HID], F32R)
        w2_t = sb("w2_t", [P, KH, DOUT])
        w2_g = sb("w2_g", [P, KH, DOUT])
        beta_b = sb("beta_b", [P, KH, P])
        w2_hi = sb("w2_hi", [P, KH, W2COLS], F32R)
        w2_lo = sb("w2_lo", [P, KH, DOUT], F32R)
        c2 = sb("c2", [P, DOUT])
        b2_half = sb("b2_half", [P, DOUT])

        adj_sb = sb("adj_sb", [P, 2, PER, P])
        w_sb = sb("w_sb", [P, 2, PER, P])
        x_sb = sb("x_sb", [P, 2, PER, DIN])
        xb_sb = sb("xb_sb", [P, 2, PER, DIN])
        h_sb = sb("h_sb", [P, PER, P], BF16)
        hw_sb = sb("hw_sb", [P, PER, P])
        degree = sb("degree", [P, 4, PER])
        hd_sb = sb("hd_sb", [P, PER, P])
        ht_sb = sb("ht_sb", [P, PER, P])
        members = sb("members", [P, PER])
        binv = sb("binv", [P, 2, PER])
        htdb_sb = sb("htdb_sb", [P, PER, P])
        at_sb = sb("at_sb", [P, 2, PER, P])
        u_hi = sb("u_hi", [P, KD, PER * P], F32R)
        u_lo = sb("u_lo", [P, KD, PER * P], F32R)
        r_sb = sb("r_sb", [P, KH, PER * P])
        r_hi = sb("r_hi", [P, KH, PER * P], F32R)
        r_lo = sb("r_lo", [P, KH, PER * P], F32R)
        sq_sb = sb("sq_sb", [P, KH, PER * P])
        pair_sb = sb("pair_sb", [P, 2, PER * P])
        q_sb = sb("q_sb", [P, PER * P])
        stat1 = sb("stat1", [P, 4, PER])
        rstd1 = sb("rstd1", [P, PER])
        g_sb = sb("g_sb", [P, PER, DOUT])
        z_sb = sb("z_sb", [P, 2, PER, DOUT])
        bn_sb = sb("bn_sb", [P, PER, 6])
        mv_sb = sb("mv_sb", [P, PER, 2])
        var2 = sb("var2", [P, PER])
        mean2 = sb("mean2", [P, PER])
        rstd2 = sb("rstd2", [P, PER])
        shift2 = sb("shift2", [P, PER])

        bank_h = ctx.enter_context(nc.psum_tensor("bank_h", [P, BANK], F32))
        bank_hd = ctx.enter_context(nc.psum_tensor("bank_hd", [P, BANK], F32))
        bank_v = ctx.enter_context(nc.psum_tensor("bank_v", [P, 2, BANK], F32))
        bank_g = ctx.enter_context(nc.psum_tensor("bank_g", [P, PER, BANK], F32))
        bank_h_bf = bank_h[:, :].bitcast(BF16)
        SUM, SQ = DOUT, 3 * P

        weights_in = [sem(f"weights_in{n}") for n in range(4)]
        adj_in = [sem("adj_in_even"), sem("adj_in_odd")]
        x_in = [sem("x_in_even"), sem("x_in_odd")]
        stored = [sem("stored_even"), sem("stored_odd")]
        consts_zeroed = sem("consts_zeroed")
        consts_ready = sem("consts_ready")
        vec_turned, vec_ready = sem("vec_turned"), sem("vec_ready")
        w1_turned, w1_hi_ready, w1_ready = sem("w1_turned"), sem("w1_hi_ready"), sem("w1_ready")
        w2_turned, w2_t_ready, w2_scaled = sem("w2_turned"), sem("w2_t_ready"), sem("w2_scaled")
        w2_summed, w2_centred, w2_hi_ready = sem("w2_summed"), sem("w2_centred"), sem("w2_hi_ready")
        w2_ready, beta_ready, c2_made = sem("w2_ready"), sem("beta_ready"), sem("c2_made")
        degree_step, d_ready = sem("degree_step"), sem("d_ready")
        hd_ready, h_turned, hd_turned = sem("hd_ready"), sem("h_turned"), sem("hd_turned")
        ht_ready, b_step, b_ready, htdb_ready = sem("ht_ready"), sem("b_step"), sem("b_ready"), sem("htdb_ready")
        at_made, at_ready = sem("at_made"), sem("at_ready")
        u_made, u_hi_ready, u_lo_ready = sem("u_made"), sem("u_hi_ready"), sem("u_lo_ready")
        v_made, relu_ready, sq_ready = sem("v_made"), sem("relu_ready"), sem("sq_ready")
        r_hi_ready, r_lo_ready = sem("r_hi_ready"), sem("r_lo_ready")
        pairs_ready, q_ready = sem("pairs_ready"), sem("q_ready")
        g_made, stat1_step, var1_ready, rstd1_ready = sem("g_made"), sem("stat1_step"), sem("var1_ready"), sem("rstd1_ready")
        g_ready, y_made = sem("g_ready"), sem("y_made")
        xb_ready, z_ready, stat2_step = sem("xb_ready"), sem("z_ready"), sem("stat2_step")
        pool_passed = sem("pool_passed")
        var2_ready, rstd2_ready, shift2_ready = sem("var2_ready"), sem("rstd2_ready"), sem("shift2_ready")
        out_ready = sem("out_ready")

        def graph(n):
            return slice(n * P, (n + 1) * P)

        def arrival(i, odd, times):
            return (i - odd) * (8 * times) + 16 * times

        def pipeline(eng, step):
            for i in range(3):
                step(i, i % 2, first=(i == 0))
            with eng.Fori(0, GROUPS // 2 - 3) as t:
                step(t * 2 + 3, 1)
                step(t * 2 + 4, 0)
            for i in range(GROUPS - 3, GROUPS):
                step(i, i % 2, ahead=min(GROUPS - 1 - i, 2))

        block = ctx.enter_context(nc.Block())

        @block.sync
        def _(sp):
            def load_adj(i, odd):
                sp.dma_start(adj_sb[:, odd], adj_dram[:, bass.ds(i * PER, PER)]).then_inc(adj_in[odd], 16)
                row = adj[bass.ds(i * PER, PER), 0, :].unsqueeze(0).to_broadcast([P, PER, P])
                sp.dma_start(w_sb[:, odd], row).then_inc(adj_in[odd], 16)

            def load_x(i, odd):
                sp.dma_start(x_sb[:, odd], x_dram[:, bass.ds(i * PER, PER)]).then_inc(x_in[odd], 16)

            def load_ahead(i, odd):
                sp.wait_ge(d_ready, i + 1)
                load_adj(i + 2, odd)
                sp.wait_ge(u_made, (i + 1) * KD)
                sp.wait_ge(xb_ready, i + 1)
                load_x(i + 2, odd)

            def store(i, odd):
                sp.wait_ge(out_ready, i + 1)
                sp.dma_start(out_dram[:, bass.ds(i * PER, PER)], z_sb[:, odd]).then_inc(stored[odd], 16)

            load_adj(0, 0)
            sp.dma_start(vec_rows[0:KH, :], b1.rearrange("(k p) -> k p", p=P)).then_inc(weights_in[0], 16)
            sp.dma_start(vec_rows[KH:2 * KH, :], gamma.rearrange("(k p) -> k p", p=P)).then_inc(weights_in[0], 16)
            sp.dma_start(vec_rows[2 * KH:3 * KH, :], beta.rearrange("(k p) -> k p", p=P)).then_inc(weights_in[0], 16)
            sp.dma_start(w1_raw[:, :, :], W1.rearrange("(k p) d -> p k d", p=P)).then_inc(weights_in[1], 16)
            load_x(0, 0)
            sp.dma_start(w2_raw[:, :, :], W2.rearrange("(k p) h -> p k h", p=P)).then_inc(weights_in[2], 16)
            sp.dma_start(b2_half[:, :], b2.unsqueeze(0).to_broadcast([P, DOUT])).then_inc(weights_in[3], 16)
            load_adj(1, 1)
            load_x(1, 1)
            load_ahead(0, 0)
            with sp.Fori(0, GROUPS // 2 - 2) as t:
                load_ahead(t * 2 + 1, 1)
                store(t * 2, 0)
                load_ahead(t * 2 + 2, 0)
                store(t * 2 + 1, 1)
            load_ahead(GROUPS - 3, 1)
            for i in range(GROUPS - 4, GROUPS):
                store(i, i % 2)
            for odd in range(2):
                sp.wait_ge(stored[odd], 8 * GROUPS)

        @block.tensor
        def _(pe):
            def turn_h(j):
                pe.wait_ge(hd_ready, j + 1)
                pe.wait_ge(at_ready, j)
                for n in range(PER):
                    mm = pe.transpose(bank_h_bf[:, graph(n)], h_sb[:, n], ident_b[:, :])
                mm.then_inc(h_turned, 1)
                pe.wait_ge(htdb_ready, j)
                for n in range(PER):
                    mm = pe.transpose(bank_hd[:, graph(n)], hd_sb[:, n], ident[:, :])
                mm.then_inc(hd_turned, 1)

            def make_at(j):
                pe.wait_ge(ht_ready, j + 1)
                pe.wait_ge(htdb_ready, j + 1)
                for n in range(PER):
                    mm = pe.matmul(bank_h[:, graph(n)], ht_sb[:, n], htdb_sb[:, n], start=True, stop=True)
                mm.then_inc(at_made, 1)

            def make_u(j, odd, bank_free):
                pe.wait_ge(at_ready, j + 1)
                pe.wait_ge(x_in[odd], arrival(j, odd, 1))
                for c in range(KD):
                    bank_free(c)
                    for n in range(PER):
                        mm = pe.matmul(bank_v[:, c, graph(n)], x_sb[:, odd, n, graph(c)], at_sb[:, odd, n],
                                       start=True, stop=True)
                    mm.then_inc(u_made, 1)

            def make_v(i, k):
                if k < 2:
                    pe.wait_ge(u_lo_ready, (i + 1) * KD)
                else:
                    pe.wait_ge(relu_ready, i * KH + (k - 1))
                terms = [(w, u, c) for w, u in ((w1_hi, u_hi), (w1_lo, u_hi), (w1_hi, u_lo)) for c in range(KD)]
                for m, (w, u, c) in enumerate(terms):
                    mm = pe.matmul(bank_v[:, k % 2], w[:, c, graph(k)], u[:, c],
                                   start=(m == 0), stop=(m == len(terms) - 1))
                mm.then_inc(v_made, 1)

            def make_g(i, n):
                for k in range(KH):
                    pe.matmul(bank_g[:, n, 0:W2COLS], r_hi[:, k, graph(n)], w2_hi[:, k], start=(k == 0), stop=False)
                    pe.matmul(bank_g[:, n, 0:DOUT], r_hi[:, k, graph(n)], w2_lo[:, k], start=False, stop=False,
                              skip_group_check=True)
                    pe.matmul(bank_g[:, n, 0:W2COLS], r_lo[:, k, graph(n)], w2_hi[:, k], start=False,
                              stop=(k == KH - 1))
                if n == 0:
                    pe.wait_ge(q_ready, i + 1)
                mm = pe.matmul(bank_g[:, n, SQ:SQ + P], q_sb[:, graph(n)], ones[:, :], start=True, stop=True)
                if n == PER - 1:
                    mm.then_inc(g_made, 1)

            def make_y(i, odd):
                pe.wait_ge(g_ready, i + 1)
                for half in range(2):
                    pe.wait_ge(relu_ready, (i + 1) * KH + 3 + half)
                    for n in range(2 * half, 2 * half + 2):
                        mm = pe.matmul(bank_v[:, half, (n % 2) * DOUT:(n % 2 + 1) * DOUT], at_sb[:, odd, n],
                                       g_sb[:, n], start=True, stop=True)
                    mm.then_inc(y_made, 1)

            pe.wait_ge(consts_ready, 2)
            pe.wait_ge(weights_in[0], 48)
            pe.transpose(bank_v[:, 0, 0:3 * KH], vec_rows[:, :], ident[0:3 * KH, 0:3 * KH]).then_inc(vec_turned, 1)
            turn_h(0)
            pe.wait_ge(weights_in[1], 16)
            for c in range(KD):
                for k in range(KH):
                    mm = pe.transpose(bank_g[:, c, graph(k)], w1_raw[:, k, graph(c)], ident[:, :])
            mm.then_inc(w1_turned, 1)
            make_at(0)
            pe.wait_ge(weights_in[2], 16)
            for k in range(KH):
                for c in range(KD):
                    mm = pe.transpose(bank_g[:, 2 + k // 2, (k % 2) * DOUT + c * P:(k % 2) * DOUT + (c + 1) * P],
                                      w2_raw[:, c, graph(k)], ident[:, :])
            mm.then_inc(w2_turned, 1)
            make_u(0, 0, lambda c: pe.wait_ge(vec_ready, 1))

            def sum_w2():
                pe.wait_ge(w2_scaled, 1)
                pe.wait_ge(consts_ready, 3)
                for k in range(KH):
                    mm = pe.matmul(bank_g[:, 0, 0:DOUT], ones[:, :], w2_g[:, k], start=(k == 0), stop=(k == KH - 1))
                mm.then_inc(w2_summed, 1)

            def make_c2():
                pe.wait_ge(beta_ready, 1)
                for k in range(KH):
                    mm = pe.matmul(bank_g[:, 1, 0:DOUT], beta_b[:, k], w2_t[:, k], start=(k == 0), stop=(k == KH - 1))
                mm.then_inc(c2_made, 1)

            def step(i, odd, first=False, ahead=2):
                if first:
                    pe.wait_ge(w1_ready, 1)
                for k in range(KH):
                    make_v(i, k)
                    if ahead and k == 1:
                        turn_h(i + 1)
                    if first and k == 2:
                        sum_w2()
                if first:
                    make_c2()
                else:
                    make_y(i - 1, 1 - odd)
                if ahead:
                    make_at(i + 1)
                pe.wait_ge(r_hi_ready, (i + 1) * KH)
                pe.wait_ge(r_lo_ready, (i + 1) * KH)
                if first:
                    pe.wait_ge(w2_ready, 1)
                make_g(i, 0)
                if ahead:
                    if first:
                        make_u(i + 1, 1 - odd, lambda c: pe.wait_ge(relu_ready, KH - 1 + c))
                    else:
                        make_u(i + 1, 1 - odd, lambda c: pe.wait_ge(z_ready, i * 2 - 1 + c))
                for n in range(1, PER):
                    make_g(i, n)

            pipeline(pe, step)
            make_y_last = GROUPS - 1
            pe.wait_ge(g_ready, GROUPS)
            for half in range(2):
                for n in range(2 * half, 2 * half + 2):
                    mm = pe.matmul(bank_v[:, half, (n % 2) * DOUT:(n % 2 + 1) * DOUT], at_sb[:, make_y_last % 2, n],
                                   g_sb[:, n], start=True, stop=True)
                mm.then_inc(y_made, 1)

        @block.scalar
        def _(act):
            def make_hd(j):
                act.wait_ge(d_ready, j + 1)
                act.wait_ge(hd_turned, j)
                for n in range(PER):
                    ins = nc.scalar.activation(hd_sb[:, n], h_sb[:, n], ACT.Copy, scale=degree[:, 3, n:n + 1])
                ins.then_inc(hd_ready, 1)

            def read_ht(j):
                act.wait_ge(h_turned, j + 1)
                act.wait_ge(at_made, j)
                act.wait_ge(b_ready, j)
                for n in range(PER):
                    ins = nc.scalar.activation(ht_sb[:, n], bank_h_bf[:, graph(n)], ACT.Copy,
                                               accum_out=members[:, n:n + 1])
                ins.then_inc(ht_ready, 1)

            def read_htdb(j):
                act.wait_ge(hd_turned, j + 1)
                act.wait_ge(b_ready, j + 1)
                for n in range(PER):
                    ins = nc.scalar.activation(htdb_sb[:, n], bank_hd[:, graph(n)], ACT.Copy,
                                               scale=binv[:, 1, n:n + 1])
                ins.then_inc(htdb_ready, 1)

            def read_at(j, odd):
                act.wait_ge(at_made, j + 1)
                nc.scalar.activation(at_sb[:, odd].rearrange("p n c -> p (n c)"), bank_h[:, :],
                                     ACT.Copy).then_inc(at_ready, 1)

            def split_u(j):
                for c in range(KD):
                    act.wait_ge(u_made, j * KD + (c + 1))
                    nc.scalar.activation(u_hi[:, c], bank_v[:, c], ACT.Copy).then_inc(u_hi_ready, 1)

            def relu(i, k, first):
                act.wait_ge(v_made, i * KH + (k + 1))
                if not first:
                    act.wait_ge(r_lo_ready, i * KH + (k + 1 - KH))
                nc.scalar.activation(r_sb[:, k], bank_v[:, k % 2], ACT.Relu,
                                     bias=vec[:, k:k + 1]).then_inc(relu_ready, 1)

            def square(i, k, first):
                act.wait_ge(relu_ready, i * KH + (k + 1))
                if not first:
                    act.wait_ge(pairs_ready, i * 2 + (k // 2 - 1))
                nc.scalar.activation(sq_sb[:, k], r_sb[:, k], ACT.Square).then_inc(sq_ready, 1)

            def normalise(i, odd):
                act.wait_ge(shift2_ready, i + 1)
                for n in range(PER):
                    ins = nc.scalar.activation(z_sb[:, odd, n], z_sb[:, odd, n], ACT.Identity,
                                               bias=shift2[:, n:n + 1], scale=rstd2[:, n:n + 1])
                ins.then_inc(out_ready, 1)

            act.wait_ge(vec_turned, 1)
            nc.scalar.activation(vec[:, :], bank_v[:, 0, 0:3 * KH], ACT.Copy).then_inc(vec_ready, 1)
            make_hd(0)
            read_ht(0)
            read_htdb(0)
            act.wait_ge(w1_turned, 1)
            nc.scalar.activation(w1_hi[:, :, :], bank_g[:, 0:KD], ACT.Copy).then_inc(w1_hi_ready, 1)
            read_at(0, 0)
            act.wait_ge(w2_turned, 1)
            nc.scalar.activation(w2_t[:, :, :].rearrange("p k o -> p (k o)"),
                                 bank_g[:, 2:4].rearrange("p b o -> p (b o)"), ACT.Copy).then_inc(w2_t_ready, 1)
            split_u(0)
            make_hd(1)
            act.wait_ge(vec_ready, 1)

            def step(i, odd, first=False, ahead=2):
                for k in range(3):
                    relu(i, k, first)
                    square(i, k, first)
                    if ahead and k == 1:
                        read_ht(i + 1)
                relu(i, 3, first)
                if ahead:
                    read_htdb(i + 1)
                square(i, 3, first)
                if first:
                    act.wait_ge(w2_centred, 1)
                    nc.scalar.activation(w2_hi[:, :, 0:DOUT], w2_g[:, :, :], ACT.Copy).then_inc(w2_hi_ready, 1)
                if ahead:
                    read_at(i + 1, 1 - odd)
                    split_u(i + 1)
                if not first:
                    normalise(i - 1, 1 - odd)
                if ahead == 2:
                    make_hd(i + 2)

            pipeline(act, step)
            normalise(GROUPS - 1, 1)

        @block.vector
        def _(dve):
            def make_d(j, odd):
                dve.wait_ge(adj_in[odd], arrival(j, odd, 2))
                dve.wait_ge(h_turned, j)
                nc.vector.tensor_scalar(h_sb[:, :, :], adj_sb[:, odd], 0.0, None, ALU.not_equal)
                for n in range(PER):
                    ins = nc.vector.scalar_tensor_tensor(out=hw_sb[:, n], in0=adj_sb[:, odd, n], scalar=0.0,
                                                         in1=w_sb[:, odd, n], op0=ALU.not_equal, op1=ALU.mult,
                                                         accum_out=degree[:, 0, n:n + 1])
                ins.then_inc(degree_step, 1)
                dve.wait_ge(degree_step, j * 3 + 1)
                nc.vector.tensor_scalar(degree[:, 1], degree[:, 0], TINY, None, ALU.max).then_inc(degree_step, 1)
                dve.wait_ge(degree_step, j * 3 + 2)
                nc.vector.reciprocal(degree[:, 2], degree[:, 1]).then_inc(degree_step, 1)
                dve.wait_ge(degree_step, j * 3 + 3)
                dve.wait_ge(hd_ready, j)
                nc.vector.scalar_tensor_tensor(out=degree[:, 3], in0=degree[:, 0], scalar=0.0, in1=degree[:, 2],
                                               op0=ALU.is_gt, op1=ALU.mult).then_inc(d_ready, 1)

            def make_b(j):
                dve.wait_ge(ht_ready, j + 1)
                nc.vector.tensor_scalar(binv[:, 0], members[:, :], 1.0, None, ALU.max).then_inc(b_step, 1)
                dve.wait_ge(b_step, j + 1)
                dve.wait_ge(htdb_ready, j)
                nc.vector.reciprocal(binv[:, 1], binv[:, 0]).then_inc(b_ready, 1)

            def split_u(j, chunks=range(KD)):
                for c in chunks:
                    dve.wait_ge(u_hi_ready, j * KD + (c + 1))
                    nc.vector.tensor_tensor(u_lo[:, c], bank_v[:, c], u_hi[:, c].bitcast(F32),
                                            ALU.subtract).then_inc(u_lo_ready, 1)

            def make_var1(i):
                dve.wait_ge(g_made, i + 1)
                nc.vector.tensor_scalar(stat1[:, 0], bank_g[:, :, SUM], 1.0 / HID, None,
                                        ALU.mult).then_inc(stat1_step, 1)
                dve.wait_ge(stat1_step, i * 3 + 1)
                nc.vector.tensor_tensor(stat1[:, 1], stat1[:, 0], stat1[:, 0], ALU.mult).then_inc(stat1_step, 1)
                dve.wait_ge(stat1_step, i * 3 + 2)
                nc.vector.scalar_tensor_tensor(out=stat1[:, 2], in0=bank_g[:, :, SQ], scalar=1.0 / HID,
                                               in1=stat1[:, 1], op0=ALU.mult,
                                               op1=ALU.subtract).then_inc(stat1_step, 1)
                dve.wait_ge(stat1_step, i * 3 + 3)
                nc.vector.tensor_scalar(stat1[:, 3], stat1[:, 2], 0.0, EPS, ALU.max,
                                        ALU.add).then_inc(var1_ready, 1)

            def read_g(i):
                dve.wait_ge(rstd1_ready, i + 1)
                if not isinstance(i, int) or i > 0:
                    dve.wait_ge(y_made, i * 2)
                for n in range(PER):
                    ins = nc.vector.scalar_tensor_tensor(out=g_sb[:, n], in0=bank_g[:, n, 0:DOUT],
                                                         scalar=rstd1[:, n:n + 1], in1=c2[:, :],
                                                         op0=ALU.mult, op1=ALU.add)
                ins.then_inc(g_ready, 1)

            def split_r(i, k):
                dve.wait_ge(r_hi_ready, i * KH + (k + 1))
                nc.vector.tensor_tensor(r_lo[:, k], r_sb[:, k], r_hi[:, k].bitcast(F32),
                                        ALU.subtract).then_inc(r_lo_ready, 1)

            def sum_pair(i, pair):
                dve.wait_ge(sq_ready, i * KH + (2 * pair + 2))
                nc.vector.tensor_tensor(pair_sb[:, pair], sq_sb[:, 2 * pair], sq_sb[:, 2 * pair + 1],
                                        ALU.add).then_inc(pairs_ready, 1)

            def make_z(i, odd, half):
                if half == 0:
                    if not isinstance(i, int) or i >= 2:
                        dve.wait_ge(stored[odd], (i - odd) * 8)
                    dve.wait_ge(xb_ready, i + 1)
                dve.wait_ge(y_made, i * 2 + (half + 1))
                pair = slice(2 * half, 2 * half + 2)
                nc.vector.scalar_tensor_tensor(out=z_sb[:, odd, pair].rearrange("p n d -> p (n d)"),
                                               in0=xb_sb[:, odd, pair].rearrange("p n d -> p (n d)"),
                                               scalar=2.0, in1=bank_v[:, half], op0=ALU.mult,
                                               op1=ALU.add).then_inc(z_ready, 1)

            def make_var2(i, odd, between=None):
                dve.wait_ge(z_ready, (i + 1) * 2)
                for n in range(PER):
                    ins = nc.vector.bn_stats(bn_sb[:, n], z_sb[:, odd, n])
                ins.then_inc(stat2_step, 1)
                dve.wait_ge(stat2_step, i * 2 + 1)
                if between:
                    between()
                for n in range(PER):
                    ins = nc.vector.bn_aggr(mv_sb[:, n], bn_sb[:, n])
                ins.then_inc(stat2_step, 1)
                dve.wait_ge(stat2_step, i * 2 + 2)
                dve.wait_ge(shift2_ready, i)
                nc.vector.tensor_scalar(mean2[:, :], mv_sb[:, :, 0], -1.0, None, ALU.mult)
                nc.vector.tensor_scalar(var2[:, :], mv_sb[:, :, 1], EPS, None, ALU.add).then_inc(var2_ready, 1)

            make_d(0, 0)
            make_b(0)
            dve.wait_ge(w1_hi_ready, 1)
            nc.vector.tensor_tensor(w1_lo[:, :, :], bank_g[:, 0:KD], w1_hi[:, :, :].bitcast(F32),
                                    ALU.subtract).then_inc(w1_ready, 1)
            split_u(0)
            make_d(1, 1)
            dve.wait_ge(w2_t_ready, 1)
            dve.wait_ge(vec_ready, 1)
            for k in range(KH):
                ins = nc.vector.tensor_scalar(w2_g[:, k], w2_t[:, k], vec[:, KH + k:KH + k + 1], None, ALU.mult)
            ins.then_inc(w2_scaled, 1)

            def centre_w2():
                dve.wait_ge(w2_summed, 1)
                for k in range(KH):
                    ins = nc.vector.scalar_tensor_tensor(out=w2_g[:, k], in0=bank_g[:, 0, 0:DOUT],
                                                         scalar=-1.0 / HID, in1=w2_g[:, k], op0=ALU.mult, op1=ALU.add)
                ins.then_inc(w2_centred, 1)

            def split_w2():
                dve.wait_ge(w2_hi_ready, 1)
                nc.vector.tensor_tensor(w2_lo[:, :, :], w2_g[:, :, :], w2_hi[:, :, 0:DOUT].bitcast(F32), ALU.subtract)
                dve.wait_ge(c2_made, 1)
                nc.vector.tensor_copy(c2[:, :], bank_g[:, 1, 0:DOUT]).then_inc(w2_ready, 1)

            def step(i, odd, first=False, ahead=2):
                if not first:
                    make_var1(i - 1)
                    read_g(i - 1)
                split_r(i, 0)
                split_r(i, 1)
                sum_pair(i, 0)
                if ahead:
                    make_b(i + 1)
                split_r(i, 2)
                if first:
                    centre_w2()
                split_r(i, 3)
                if not first:
                    make_z(i - 1, 1 - odd, 0)
                sum_pair(i, 1)
                dve.wait_ge(pairs_ready, i * 2 + 2)
                nc.vector.tensor_tensor(q_sb[:, :], pair_sb[:, 0], pair_sb[:, 1], ALU.add).then_inc(q_ready, 1)
                if first:
                    split_w2()
                    split_u(i + 1)
                else:
                    make_z(i - 1, 1 - odd, 1)
                    if ahead:
                        make_var2(i - 1, 1 - odd, between=lambda: split_u(i + 1, [0]))
                        split_u(i + 1, [1])
                    else:
                        make_var2(i - 1, 1 - odd)
                if ahead == 2:
                    make_d(i + 2, odd)

            pipeline(dve, step)
            make_var1(GROUPS - 1)
            read_g(GROUPS - 1)
            for half in range(2):
                make_z(GROUPS - 1, 1, half)
            make_var2(GROUPS - 1, 1)

        @block.gpsimd
        def _(pool):
            nc.gpsimd.memset(ident[:, :], 0.0).then_inc(consts_zeroed, 1)
            nc.gpsimd.memset(ident_b[:, :], 0.0).then_inc(consts_zeroed, 1)
            for n, m in enumerate((ident, ident_b)):
                pool.wait_ge(consts_zeroed, n + 1)
                nc.gpsimd.affine_select(out=m[:, :], in_=m[:, :], compare_op=ALU.not_equal, fill=1.0, base=0,
                                        pattern=[[-1, P]], channel_multiplier=1).then_inc(consts_ready, 1)
            nc.gpsimd.memset(half_power[:, :], -0.5)
            nc.gpsimd.memset(w2_hi[:, :, DOUT:W2COLS].bitcast(F32), 1.0)
            nc.gpsimd.memset(ones[:, :], 1.0).then_inc(consts_ready, 1)
            pool.wait_ge(consts_ready, 3)
            pool.wait_ge(vec_ready, 1)
            for k in range(KH):
                ins = nc.gpsimd.tensor_scalar(beta_b[:, k], ones[:, :], vec[:, 2 * KH + k:2 * KH + k + 1], 1.0,
                                              ALU.mult, ALU.mult)
            ins.then_inc(beta_ready, 1)
            pool.wait_ge(weights_in[3], 16)
            nc.gpsimd.tensor_scalar(b2_half[:, :], b2_half[:, :], 0.5, 1.0, ALU.mult,
                                    ALU.mult).then_inc(consts_ready, 1)
            pool.wait_ge(consts_ready, 4)

            def inverse_std1(i):
                pool.wait_ge(var1_ready, i + 1)
                nc.gpsimd.tensor_tensor(rstd1[:, :], stat1[:, 3], half_power[:, :], ALU.pow).then_inc(rstd1_ready, 1)

            def add_b2(i, odd, y_before):
                pool.wait_ge(x_in[odd], arrival(i, odd, 1))
                if y_before is not None:
                    pool.wait_ge(z_ready, y_before)
                nc.gpsimd.tensor_tensor(xb_sb[:, odd], x_sb[:, odd],
                                        b2_half[:, :].unsqueeze(1).to_broadcast([P, PER, DOUT]),
                                        ALU.add).then_inc(xb_ready, 1)

            def split_r(i, k):
                pool.wait_ge(relu_ready, i * KH + (k + 1))
                pool.sem_inc(pool_passed, 1)
                nc.gpsimd.tensor_scalar(r_hi[:, k], r_sb[:, k], 1.0, 1.0, ALU.mult, ALU.mult).then_inc(r_hi_ready, 1)

            def inverse_std2(i):
                pool.wait_ge(var2_ready, i + 1)
                pool.wait_ge(out_ready, i)
                nc.gpsimd.tensor_tensor(rstd2[:, :], var2[:, :], half_power[:, :], ALU.pow).then_inc(rstd2_ready, 1)
                pool.wait_ge(rstd2_ready, i + 1)
                nc.gpsimd.tensor_tensor(shift2[:, :], mean2[:, :], rstd2[:, :], ALU.mult).then_inc(shift2_ready, 1)

            def step(i, odd, first=False, ahead=2):
                if not first:
                    inverse_std1(i - 1)
                for k in range(KH):
                    split_r(i, k)
                add_b2(i, odd, None if first else i * 2 - 2)
                if not first:
                    inverse_std2(i - 1)

            pipeline(pool, step)
            inverse_std1(GROUPS - 1)
            inverse_std2(GROUPS - 1)


_INS = ["x", "adj", "L0_gnn_W1", "L0_gnn_b1", "L0_gnn_gamma", "L0_gnn_beta", "L0_gnn_W2", "L0_gnn_b2"]


def kernel(**inputs):
    import numpy as _np
    import concourse.bacc as _bacc
    from concourse import mybir as _mybir
    from concourse.bass_utils import run_bass_kernel_spmd as _run

    nc = _bacc.Bacc("TRN2", target_bir_lowering=False, num_devices=1)
    arrays, args = {}, []
    for name in _INS:
        a = _np.ascontiguousarray(inputs[name])
        arrays[f"in_{name}_dram"] = a
        args.append(nc.dram_tensor(f"in_{name}_dram", a.shape, _mybir.dt.from_np(a.dtype), kind="ExternalInput").ap())
    args.append(nc.dram_tensor("out_dram", inputs["x"].shape, _mybir.dt.float32, kind="ExternalOutput").ap())
    hypergraph_block(nc, *args)
    r = _run(nc, [arrays], core_ids=[0])
    return r.results[0]["out_dram"]
```

```python
from contextlib import ExitStack

import concourse.bass as bass
from concourse import mybir

ALU = mybir.AluOpType
ACT = mybir.ActivationFunctionType
AX = mybir.AxisListType
F32 = mybir.dt.float32
F32R = mybir.dt.float32r
BF16 = mybir.dt.bfloat16

P = 128
PER = 4
BANK = 512
EPS = 1e-5
WARM_UP = 26
TINY = 1.1754944e-38


def hypergraph_block(nc, x, adj, W1, b1, gamma, beta, W2, b2, out):
    N, C, DIN = x.shape
    HID = W1.shape[0]
    DOUT = W2.shape[0]
    KD, KH = DIN // P, HID // P
    GROUPS = N // PER
    assert C == P and DIN == DOUT == 2 * P and HID == BANK and GROUPS % 2 == 0
    W2COLS = DOUT + 2

    x_dram = x.rearrange("n c d -> c n d")
    adj_dram = adj.rearrange("n c e -> c n e")
    out_dram = out.rearrange("n c d -> c n d")

    with ExitStack() as ctx:
        def sb(name, shape, dt=F32):
            return ctx.enter_context(nc.sbuf_tensor(name, shape, dt))

        def sem(name):
            return ctx.enter_context(nc.semaphore(name))

        ident = sb("ident", [P, P])
        ident_b = sb("ident_b", [P, P], BF16)
        ones = sb("ones", [P, P])
        ident_2 = sb("ident_2", [P, P])
        half_power = sb("half_power", [P, PER])
        w1_raw = sb("w1_raw", [P, KH, DIN])
        w2_raw = sb("w2_raw", [P, KD, HID])
        vec_rows = sb("vec_rows", [3 * KH, P])
        vec = sb("vec", [P, 3 * KH])
        w1_hi = sb("w1_hi", [P, KD, HID], F32R)
        w1_lo = sb("w1_lo", [P, KD, HID], F32R)
        w2_t = sb("w2_t", [P, KH, DOUT])
        w2_g = sb("w2_g", [P, KH, DOUT])
        w2_sum = sb("w2_sum", [P, KH // 2, DOUT])
        beta_b = sb("beta_b", [P, KH, P])
        w2_hi = sb("w2_hi", [P, KH, W2COLS], F32R)
        w2_lo = sb("w2_lo", [P, KH, DOUT], F32R)
        c2 = sb("c2", [P, DOUT])
        b2_half = sb("b2_half", [P, DOUT])

        adj_sb = sb("adj_sb", [P, 2, PER, P])
        w_sb = sb("w_sb", [P, 2, PER, P])
        x_sb = sb("x_sb", [P, 2, PER, DIN])
        xb_sb = sb("xb_sb", [P, 2, PER, DIN])
        h_sb = sb("h_sb", [P, PER, P], BF16)
        hw_sb = sb("hw_sb", [P, PER, P])
        degree = sb("degree", [P, 4, PER])
        drow_sb = sb("drow_sb", [P, 2, PER, P])
        diag_sb = sb("diag_sb", [P, PER, P])
        ht_sb = sb("ht_sb", [P, PER, P])
        members = sb("members", [P, PER])
        binv = sb("binv", [P, 2, PER])
        htb_sb = sb("htb_sb", [P, PER, P])
        at_sb = sb("at_sb", [P, PER, P])
        at_hi = sb("at_hi", [P, 2, PER, P], F32R)
        at_lo = sb("at_lo", [P, 2, PER, P], F32R)
        u_hi = sb("u_hi", [P, KD, PER * P], F32R)
        u_lo = sb("u_lo", [P, KD, PER * P], F32R)
        r_sb = sb("r_sb", [P, KH, PER * P])
        r_hi = sb("r_hi", [P, KH, PER * P], F32R)
        r_lo = sb("r_lo", [P, KH, PER * P], F32R)
        sq_sb = sb("sq_sb", [P, KH, PER * P])
        pair_sb = sb("pair_sb", [P, 2, PER * P])
        q_sb = sb("q_sb", [P, PER * P])
        scratch = sb("scratch", [P, PER, P])
        sum_sq = sb("sum_sq", [P, PER])
        stat1 = sb("stat1", [P, 4, PER])
        rstd1 = sb("rstd1", [P, PER])
        g_sb = sb("g_sb", [P, PER, DOUT])
        g_hi = sb("g_hi", [P, PER, DOUT], F32R)
        g_lo = sb("g_lo", [P, PER, DOUT], F32R)
        z_sb = sb("z_sb", [P, 2, PER, DOUT])
        bn_sb = sb("bn_sb", [P, PER, 6])
        mv_sb = sb("mv_sb", [P, 2, PER, 2])
        var2 = sb("var2", [P, 2, PER])
        mean2 = sb("mean2", [P, 2, PER])
        rstd2 = sb("rstd2", [P, 2, PER])
        shift2 = sb("shift2", [P, PER])

        bank_h = ctx.enter_context(nc.psum_tensor("bank_h", [P, BANK], F32))
        bank_q = ctx.enter_context(nc.psum_tensor("bank_q", [P, BANK], F32))
        bank_v = ctx.enter_context(nc.psum_tensor("bank_v", [P, 2, BANK], F32))
        bank_g = ctx.enter_context(nc.psum_tensor("bank_g", [P, PER, BANK], F32))
        bank_h_bf = bank_h[:, :].bitcast(BF16)
        last_z = [bank[:, 0:DOUT] for bank in (bank_v[:, 0], bank_v[:, 1], bank_h, bank_q)]
        SUM = DOUT

        weights_in = [sem(f"weights_in{n}") for n in range(4)]
        adj_in = [sem("adj_in_even"), sem("adj_in_odd")]
        x_in = [sem("x_in_even"), sem("x_in_odd")]
        stored = [sem("stored_even"), sem("stored_odd")]
        consts_zeroed = sem("consts_zeroed")
        consts_ready = sem("consts_ready")
        vec_turned, vec_ready = sem("vec_turned"), sem("vec_ready")
        w1_turned, w1_hi_ready, w1_ready = sem("w1_turned"), sem("w1_hi_ready"), sem("w1_ready")
        w2_turned, w2_t_ready, w2_scaled = sem("w2_turned"), sem("w2_t_ready"), sem("w2_scaled")
        w2_added = sem("w2_added")
        w2_summed, w2_centred, w2_hi_ready = sem("w2_summed"), sem("w2_centred"), sem("w2_hi_ready")
        w2_ready, beta_ready, c2_made = sem("w2_ready"), sem("beta_ready"), sem("c2_made")
        c2_ready = sem("c2_ready")
        degree_summed, hw_ready = sem("degree_summed"), sem("hw_ready")
        degree_step, d_ready = sem("degree_step"), sem("d_ready")
        diag_ready, diag_summed, drow0_ready = sem("diag_ready"), sem("diag_summed"), sem("drow0_ready")
        rows_stored = sem("rows_stored")
        drow_in = [sem("drow_in_even"), sem("drow_in_odd")]
        h_turned = sem("h_turned")
        ht_ready, b_step, b_ready, htb_ready = sem("ht_ready"), sem("b_step"), sem("b_ready"), sem("htb_ready")
        h_ready, at_made, at_ready = sem("h_ready"), sem("at_made"), sem("at_ready")
        at_hi_ready, at_lo_ready = sem("at_hi_ready"), sem("at_lo_ready")
        g_hi_ready, g_lo_ready = sem("g_hi_ready"), sem("g_lo_ready")
        u_made, u_hi_ready, u_lo_ready = sem("u_made"), sem("u_hi_ready"), sem("u_lo_ready")
        v_made, relu_ready, sq_ready = sem("v_made"), sem("relu_ready"), sem("sq_ready")
        r_hi_ready, r_lo_ready = sem("r_hi_ready"), sem("r_lo_ready")
        pairs_ready = sem("pairs_ready")
        q_ready, q_turned, q_summed = sem("q_ready"), sem("q_turned"), sem("q_summed")
        g_made, stat1_step, var1_ready, rstd1_ready = sem("g_made"), sem("stat1_step"), sem("var1_ready"), sem("rstd1_ready")
        g_ready, y_made = sem("g_ready"), sem("y_made")
        xb_ready, z_ready = sem("xb_ready"), sem("z_ready")
        stats_ready, mean2_ready = sem("stats_ready"), sem("mean2_ready")
        pool_passed = sem("pool_passed")
        vector_passed = sem("vector_passed")
        var2_ready, rstd2_ready, shift2_ready = sem("var2_ready"), sem("rstd2_ready"), sem("shift2_ready")
        out_ready, last_out_ready = sem("out_ready"), sem("last_out_ready")

        def graph(n):
            return slice(n * P, (n + 1) * P)

        def graphs(half):
            return slice(0, PER) if half is None else slice(half * (PER // 2), (half + 1) * (PER // 2))

        def each(half):
            return range(PER)[graphs(half)]

        def arrival(i, odd, times):
            return (i - odd) * (8 * times) + 16 * times

        def pipeline(eng, step):
            for i in range(3):
                step(i, i % 2, first=(i == 0))
            with eng.Fori(0, GROUPS // 2 - 3) as t:
                step(t * 2 + 3, 1)
                step(t * 2 + 4, 0)
            for i in range(GROUPS - 3, GROUPS):
                step(i, i % 2, ahead=min(GROUPS - 1 - i, 2))

        d_rows = nc.dram_tensor("d_rows", [GROUPS, PER, P], F32, kind="Internal").ap()

        block = ctx.enter_context(nc.Block())

        @block.sync
        def _(sp):
            def load_adj(i, odd):
                sp.dma_start(adj_sb[:, odd], adj_dram[:, bass.ds(i * PER, PER)]).then_inc(adj_in[odd], 16)
                if isinstance(i, int) and i == 0:
                    return
                row = adj[bass.ds(i * PER, PER), 0, :].unsqueeze(0).to_broadcast([P, PER, P])
                sp.dma_start(w_sb[:, odd], row).then_inc(adj_in[odd], 16)

            def load_x(i, odd):
                sp.dma_start(x_sb[:, odd], x_dram[:, bass.ds(i * PER, PER)]).then_inc(x_in[odd], 16)

            def load_x_ahead(i, odd):
                sp.wait_ge(u_made, (i - 1) * KD)
                sp.wait_ge(xb_ready, i - 1)
                load_x(i, odd)

            def turn_d(j, odd, load=True):
                sp.wait_ge(d_ready, j + 1)
                with nc.allow_non_contiguous_dma(reason="2 KB in all"):
                    sp.dma_start(d_rows[bass.ds(j, 1)].rearrange("o n c -> c (o n)"),
                                 degree[:, 3]).then_inc(rows_stored, 16)
                if load:
                    load_adj(j + 2, odd)
                sp.wait_ge(rows_stored, j * 16)
                sp.dma_start(drow_sb[:, odd], d_rows[bass.ds(j, 1)].to_broadcast([P, PER, P])).then_inc(drow_in[odd], 16)

            def store(i, odd, half=None):
                part, n = graphs(half), len(each(half))
                if half is None:
                    sp.wait_ge(out_ready, i + 1)
                else:
                    sp.wait_ge(last_out_ready, half + 1)
                sp.dma_start(out_dram[:, bass.ds(i * PER + part.start, n)],
                             z_sb[:, odd, part]).then_inc(stored[odd], 16)

            load_adj(0, 0)
            sp.dma_start(w1_raw[:, :, :], W1.rearrange("(k p) d -> p k d", p=P)).then_inc(weights_in[1], 16)
            sp.dma_start(w2_raw[:, :, :], W2.rearrange("(k p) h -> p k h", p=P)).then_inc(weights_in[2], 16)
            load_x(0, 0)
            load_adj(1, 1)
            sp.dma_start(b2_half[:, :], b2.unsqueeze(0).to_broadcast([P, DOUT])).then_inc(weights_in[3], 16)
            load_x(1, 1)
            sp.wait_ge(d_ready, 1)
            load_adj(2, 0)
            turn_d(1, 1)

            def step(i, odd, adj_left=True):
                if not isinstance(i, int) or i < GROUPS - 2:
                    load_x_ahead(i + 2, odd)
                if not isinstance(i, int) or i < GROUPS - 2:
                    turn_d(i + 2, odd, load=adj_left)
                if not isinstance(i, int) or i >= 2:
                    store(i - 2, odd)

            step(0, 0)
            step(1, 1)
            with sp.Fori(0, GROUPS // 2 - 3) as t:
                step(t * 2 + 2, 0)
                step(t * 2 + 3, 1)
            for i in range(GROUPS - 4, GROUPS):
                step(i, i % 2, adj_left=False)
            store(GROUPS - 2, 0)
            for half in range(2):
                store(GROUPS - 1, 1, half)
            sp.wait_ge(stored[0], 8 * GROUPS)
            sp.wait_ge(stored[1], 8 * GROUPS + 16)

        @block.tensor
        def _(pe):
            def turn_h(j):
                pe.wait_ge(h_ready, j + 1)
                if not isinstance(j, int) or j >= 1:
                    pe.wait_ge(at_ready, j)
                for n in range(PER):
                    mm = pe.transpose(bank_h_bf[:, graph(n)], h_sb[:, n], ident_b[:, :])
                mm.then_inc(h_turned, 1)

            def make_at(j):
                pe.wait_ge(ht_ready, j + 1)
                pe.wait_ge(htb_ready, j + 1)
                for n in range(PER):
                    mm = pe.matmul(bank_h[:, graph(n)], ht_sb[:, n], htb_sb[:, n], start=True, stop=True)
                mm.then_inc(at_made, 1)

            def make_u(j, odd, bank_free):
                pe.wait_ge(at_ready, j + 1)
                pe.wait_ge(x_in[odd], arrival(j, odd, 1))
                for c in range(KD):
                    bank_free(c)
                    for n in range(PER):
                        mm = pe.matmul(bank_v[:, c, graph(n)], x_sb[:, odd, n, graph(c)], at_sb[:, n],
                                       start=True, stop=True)
                    mm.then_inc(u_made, 1)

            def make_v(i, k):
                if k < 2:
                    pe.wait_ge(u_lo_ready, i * KD + (k + 1))
                else:
                    pe.wait_ge(relu_ready, i * KH + (k - 1))
                terms = [(w, u, c) for c in range(KD) for w, u in ((w1_hi, u_hi), (w1_lo, u_hi), (w1_hi, u_lo))]
                for m, (w, u, c) in enumerate(terms):
                    if k == 0 and m == len(terms) // KD:
                        pe.wait_ge(u_hi_ready, (i + 1) * KD)
                    if k == 0 and m == len(terms) - 1:
                        pe.wait_ge(u_lo_ready, (i + 1) * KD)
                    mm = pe.matmul(bank_v[:, k % 2], w[:, c, graph(k)], u[:, c],
                                   start=(m == 0), stop=(m == len(terms) - 1))
                mm.then_inc(v_made, 1)

            def start_g(i, n, chunks=range(KH)):
                for k in chunks:
                    pe.matmul(bank_g[:, n, 0:W2COLS], r_hi[:, k, graph(n)], w2_hi[:, k], start=(k == 0), stop=False)
                    pe.matmul(bank_g[:, n, 0:DOUT], r_hi[:, k, graph(n)], w2_lo[:, k], start=False, stop=False,
                              skip_group_check=True)

            def finish_g(i, n, last=False):
                if n == 0:
                    pe.wait_ge(r_lo_ready, (i + 1) * KH)
                for k in range(KH):
                    mm = pe.matmul(bank_g[:, n, 0:W2COLS], r_lo[:, k, graph(n)], w2_hi[:, k], start=False,
                                   stop=(k == KH - 1))
                if n == PER - 1 or (last and n == PER // 2 - 1):
                    mm.then_inc(g_made, 1)

            def turn_q(i):
                pe.wait_ge(q_ready, i + 1)
                if isinstance(i, int) and i == 0:
                    pe.wait_ge(drow0_ready, 1)
                else:
                    pe.wait_ge(q_summed, i)
                for n in range(PER):
                    mm = pe.transpose(bank_q[:, graph(n)], q_sb[:, graph(n)], ident[:, :])
                mm.then_inc(q_turned, 1)

            def make_y(i, odd, half, bank_free):
                pe.wait_ge(at_lo_ready, i + 1)
                pe.wait_ge(g_lo_ready, i * 2 + (half + 1))
                bank_free()
                for n in each(half):
                    for m, (a, g) in enumerate(((at_hi, g_hi), (at_hi, g_lo), (at_lo, g_hi))):
                        mm = pe.matmul(bank_v[:, half, (n % 2) * DOUT:(n % 2 + 1) * DOUT], a[:, odd, n], g[:, n],
                                       start=(m == 0), stop=(m == 2))
                mm.then_inc(y_made, 1)

            pe.wait_ge(consts_ready, 2)
            for _ in range(WARM_UP):
                pe.transpose(bank_q[:, :].bitcast(BF16)[:, graph(0)], ident_b[:, :], ident_b[:, :])
            turn_h(0)
            pe.wait_ge(weights_in[1], 16)
            for c in range(KD):
                for k in range(KH):
                    mm = pe.transpose(bank_g[:, c, graph(k)], w1_raw[:, k, graph(c)], ident[:, :])
            mm.then_inc(w1_turned, 1)
            pe.wait_ge(consts_ready, 3)
            pe.wait_ge(diag_ready, 1)
            pe.matmul(bank_q[:, :], ones[:, :], diag_sb[:, :, :], start=True, stop=True).then_inc(diag_summed, 1)
            make_at(0)
            pe.wait_ge(weights_in[2], 16)
            for k in range(KH):
                for c in range(KD):
                    mm = pe.transpose(bank_g[:, 2 + k // 2, (k % 2) * DOUT + c * P:(k % 2) * DOUT + (c + 1) * P],
                                      w2_raw[:, c, graph(k)], ident[:, :])
            mm.then_inc(w2_turned, 1)
            pe.wait_ge(weights_in[0], 48)
            pe.transpose(bank_v[:, 0, 0:3 * KH], vec_rows[:, :], ident[0:3 * KH, 0:3 * KH]).then_inc(vec_turned, 1)
            make_u(0, 0, lambda c: pe.wait_ge(vec_ready, 1))

            def sum_w2():
                pe.wait_ge(w2_added, 2)
                mm = pe.matmul(bank_g[:, 0, 0:DOUT], ones[:, :], w2_sum[:, 0], start=True, stop=True)
                mm.then_inc(w2_summed, 1)

            def make_c2():
                pe.wait_ge(beta_ready, 1)
                pe.wait_ge(w2_t_ready, 1)
                for k in range(KH):
                    mm = pe.matmul(bank_g[:, 1, 0:DOUT], beta_b[:, k], w2_t[:, k], start=(k == 0), stop=(k == KH - 1))
                mm.then_inc(c2_made, 1)

            def step(i, odd, first=False, ahead=2):
                if ahead:
                    turn_h(i + 1)
                for k in range(KH):
                    if first and k == 0:
                        pe.wait_ge(w1_ready, 1)
                    make_v(i, k)
                    if first and k == 1:
                        sum_w2()
                    if ahead and k == (KH - 1 if first else 2):
                        make_at(i + 1)
                if first:
                    make_c2()
                    pe.wait_ge(r_hi_ready, KH // 2)
                    pe.wait_ge(w2_ready, 1)
                    start_g(i, 0, range(KH // 2))
                else:
                    make_y(i - 1, 1 - odd, 0, lambda: pe.wait_ge(relu_ready, i * KH + 3))
                    pe.wait_ge(r_hi_ready, i * KH + 2)
                    start_g(i, 0, range(KH // 2))
                    make_y(i - 1, 1 - odd, 1, lambda: pe.wait_ge(relu_ready, i * KH + 4))
                pe.wait_ge(r_hi_ready, (i + 1) * KH)
                start_g(i, 0, range(KH // 2, KH))
                if not first:
                    start_g(i, 1)
                finish_g(i, 0)
                if ahead:
                    if first:
                        make_u(i + 1, 1 - odd, lambda c: pe.wait_ge(relu_ready, KH - 1 + c))
                    else:
                        make_u(i + 1, 1 - odd, lambda c: pe.wait_ge(z_ready, i * 2 - 1 + c))
                if first:
                    pe.wait_ge(c2_ready, 1)
                    start_g(i, 1)
                finish_g(i, 1, last=not ahead)
                start_g(i, 2, range(KH // 2))
                if not ahead:
                    turn_q(i)
                start_g(i, 2, range(KH // 2, KH))
                if ahead:
                    turn_q(i)
                finish_g(i, 2)
                start_g(i, 3)
                finish_g(i, 3)

            pipeline(pe, step)
            pe.wait_ge(consts_ready, 5)
            pe.wait_ge(xb_ready, GROUPS)
            for n in range(PER):
                if n < 2:
                    pe.wait_ge(z_ready, (GROUPS - 1) * 2 - 1 + n)
                elif n == 3:
                    pe.wait_ge(q_summed, GROUPS)
                pe.matmul(last_z[n], ident_2[:, :], xb_sb[:, 1, n], start=True, stop=False)
            for half in range(2):
                pe.wait_ge(g_ready, (GROUPS - 1) * 2 + half + 1)
                for n in each(half):
                    mm = pe.matmul(last_z[n], at_sb[:, n], g_sb[:, n], start=False, stop=True)
                mm.then_inc(y_made, 1)

        @block.scalar
        def _(act):
            def sum_degree(j):
                act.wait_ge(hw_ready, j)
                act.wait_ge(d_ready, j)
                for n in range(PER):
                    ins = nc.scalar.activation(hw_sb[:, n], hw_sb[:, n], ACT.Copy,
                                               accum_out=degree[:, 0, n:n + 1])
                ins.then_inc(degree_summed, 1)

            def read_ht(j):
                act.wait_ge(h_turned, j + 1)
                act.wait_ge(at_made, j)
                act.wait_ge(b_ready, j)
                for n in range(PER):
                    ins = nc.scalar.activation(ht_sb[:, n], bank_h_bf[:, graph(n)], ACT.Copy,
                                               accum_out=members[:, n:n + 1])
                ins.then_inc(ht_ready, 1)

            def make_htb(j):
                act.wait_ge(b_ready, j + 1)
                act.wait_ge(at_made, j)
                for n in range(PER):
                    ins = nc.scalar.activation(htb_sb[:, n], ht_sb[:, n], ACT.Copy, scale=binv[:, 1, n:n + 1])
                ins.then_inc(htb_ready, 1)

            def read_at_hi(j, odd):
                act.wait_ge(at_ready, j + 1)
                if not isinstance(j, int) or j >= 2:
                    act.wait_ge(y_made, (j - 1) * 2)
                nc.scalar.activation(at_hi[:, odd].rearrange("p n c -> p (n c)"),
                                     at_sb[:, :, :].rearrange("p n c -> p (n c)"), ACT.Copy).then_inc(at_hi_ready, 1)

            def split_u(j):
                for c in range(KD):
                    act.wait_ge(u_made, j * KD + (c + 1))
                    nc.scalar.activation(u_hi[:, c], bank_v[:, c], ACT.Copy).then_inc(u_hi_ready, 1)

            def relu(i, k, first):
                act.wait_ge(v_made, i * KH + (k + 1))
                if not first:
                    act.wait_ge(r_lo_ready, i * KH + (k + 1 - KH))
                nc.scalar.activation(r_sb[:, k], bank_v[:, k % 2], ACT.Relu,
                                     bias=vec[:, k:k + 1]).then_inc(relu_ready, 1)

            def square(i, k, first):
                act.wait_ge(relu_ready, i * KH + (k + 1))
                if not first:
                    act.wait_ge(pairs_ready, i * 2 - k // 2)
                nc.scalar.activation(sq_sb[:, k], r_sb[:, k], ACT.Square).then_inc(sq_ready, 1)

            def normalise(i, odd):
                act.wait_ge(shift2_ready, i + 1)
                for n in range(PER):
                    ins = nc.scalar.activation(z_sb[:, odd, n], z_sb[:, odd, n], ACT.Identity,
                                               bias=shift2[:, n:n + 1], scale=rstd2[:, 0, n:n + 1])
                ins.then_inc(out_ready, 1)

            def sum_q(i):
                act.wait_ge(q_turned, i + 1)
                if not isinstance(i, int) or i >= 1:
                    act.wait_ge(var1_ready, i)
                for n in range(PER):
                    ins = nc.scalar.activation(scratch[:, n], bank_q[:, graph(n)], ACT.Copy,
                                               accum_out=sum_sq[:, n:n + 1])
                ins.then_inc(q_summed, 1)

            row = adj[0:PER, 0, :].unsqueeze(0).to_broadcast([P, PER, P])
            act.dma_start(w_sb[:, 0], row).then_inc(adj_in[0], 16)
            for n, v in enumerate((b1, gamma, beta)):
                act.dma_start(vec_rows[n * KH:(n + 1) * KH, :],
                              v.rearrange("(k p) -> k p", p=P)).then_inc(weights_in[0], 16)
            read_ht(0)
            make_htb(0)
            act.wait_ge(diag_summed, 1)
            nc.scalar.activation(drow_sb[:, 0].rearrange("p n c -> p (n c)"), bank_q[:, :],
                                 ACT.Copy).then_inc(drow0_ready, 1)
            act.wait_ge(w1_turned, 1)
            nc.scalar.activation(w1_hi[:, :, :], bank_g[:, 0:KD], ACT.Copy).then_inc(w1_hi_ready, 1)
            act.wait_ge(vec_turned, 1)
            nc.scalar.activation(vec[:, :], bank_v[:, 0, 0:3 * KH], ACT.Copy).then_inc(vec_ready, 1)
            read_at_hi(0, 0)
            split_u(0)
            sum_degree(1)
            act.wait_ge(vec_ready, 1)

            def step(i, odd, first=False, ahead=2):
                if ahead and not first:
                    read_ht(i + 1)
                relu(i, 0, first)
                if first:
                    read_ht(1)
                elif ahead:
                    make_htb(i + 1)
                else:
                    square(i, 0, first)
                relu(i, 1, first)
                if first:
                    make_htb(1)
                    act.wait_ge(w2_scaled, 2)
                    nc.scalar.activation(w2_t[:, :, :].rearrange("p k o -> p (k o)"),
                                         bank_g[:, 2:4].rearrange("p b o -> p (b o)"), ACT.Copy).then_inc(w2_t_ready, 1)
                    act.wait_ge(w2_centred, 1)
                    nc.scalar.activation(w2_hi[:, :, 0:DOUT], w2_g[:, :, :], ACT.Copy).then_inc(w2_hi_ready, 1)
                if not first:
                    square(i, 1, first)
                relu(i, 2, first)
                if not first:
                    square(i, 2, first)
                relu(i, 3, first)
                if first:
                    square(i, 1, first)
                    square(i, 2, first)
                square(i, 3, first)
                if ahead:
                    square(i, 0, first)
                if ahead:
                    read_at_hi(i + 1, 1 - odd)
                if not isinstance(i, int) or i >= 2:
                    normalise(i - 2, odd)
                if ahead:
                    split_u(i + 1)
                if ahead == 2:
                    sum_degree(i + 2)
                sum_q(i)

            pipeline(act, step)
            normalise(GROUPS - 2, 0)

        @block.vector
        def _(dve):
            def make_h(j, odd):
                dve.wait_ge(adj_in[odd], arrival(j, odd, 2))
                dve.wait_ge(h_turned, j)
                dve.wait_ge(degree_summed, j)
                nc.vector.tensor_scalar(h_sb[:, :, :], adj_sb[:, odd], 0.0, None,
                                        ALU.not_equal).then_inc(h_ready, 1)

            def guard_d(j):
                dve.wait_ge(degree_summed, j + 1)
                nc.vector.tensor_scalar(degree[:, 1], degree[:, 0], TINY, None, ALU.max).then_inc(degree_step, 1)

            def invert_d(j):
                dve.wait_ge(degree_step, j * 2 + 1)
                nc.vector.reciprocal(degree[:, 2], degree[:, 1]).then_inc(degree_step, 1)

            def select_d(j):
                dve.wait_ge(degree_step, j * 2 + 2)
                if not isinstance(j, int) or j >= 2:
                    dve.wait_ge(rows_stored, (j - 1) * 16)
                elif j == 1:
                    dve.wait_ge(diag_ready, 1)
                nc.vector.scalar_tensor_tensor(out=degree[:, 3], in0=degree[:, 0], scalar=0.0, in1=degree[:, 2],
                                               op0=ALU.is_gt, op1=ALU.mult).then_inc(d_ready, 1)

            def make_d(j):
                guard_d(j)
                invert_d(j)
                select_d(j)

            def make_b(j):
                dve.wait_ge(ht_ready, j + 1)
                nc.vector.tensor_scalar(binv[:, 0], members[:, :], 1.0, None, ALU.max).then_inc(b_step, 1)
                dve.wait_ge(b_step, j + 1)
                dve.wait_ge(htb_ready, j)
                nc.vector.reciprocal(binv[:, 1], binv[:, 0]).then_inc(b_ready, 1)

            def make_at_sb(j, odd):
                dve.wait_ge(at_made, j + 1)
                if isinstance(j, int) and j == 0:
                    dve.wait_ge(drow0_ready, 1)
                else:
                    dve.wait_ge(drow_in[odd], (j + odd) * 8)
                    dve.wait_ge(at_lo_ready, j)
                nc.vector.tensor_tensor(at_sb[:, :, :].rearrange("p n c -> p (n c)"), bank_h[:, :],
                                        drow_sb[:, odd].rearrange("p n c -> p (n c)"), ALU.mult).then_inc(at_ready, 1)

            def split_u(j, chunks=range(KD)):
                for c in chunks:
                    dve.wait_ge(u_hi_ready, j * KD + (c + 1))
                    nc.vector.tensor_tensor(u_lo[:, c], bank_v[:, c], u_hi[:, c].bitcast(F32),
                                            ALU.subtract).then_inc(u_lo_ready, 1)

            def make_var1(i, half=None):
                part, done = graphs(half), i + (half or 0)
                dve.wait_ge(g_made, done + 1)
                nc.vector.tensor_scalar(stat1[:, 0, part], bank_g[:, part, SUM], 1.0 / HID, None,
                                        ALU.mult).then_inc(stat1_step, 1)
                dve.wait_ge(stat1_step, done * 3 + 1)
                nc.vector.tensor_tensor(stat1[:, 1, part], stat1[:, 0, part], stat1[:, 0, part],
                                        ALU.mult).then_inc(stat1_step, 1)
                dve.wait_ge(q_summed, i + 1)
                dve.wait_ge(stat1_step, done * 3 + 2)
                nc.vector.scalar_tensor_tensor(out=stat1[:, 2, part], in0=sum_sq[:, part], scalar=1.0 / HID,
                                               in1=stat1[:, 1, part], op0=ALU.mult,
                                               op1=ALU.subtract).then_inc(stat1_step, 1)
                dve.wait_ge(stat1_step, done * 3 + 3)
                nc.vector.tensor_scalar(stat1[:, 3, part], stat1[:, 2, part], 0.0, EPS, ALU.max,
                                        ALU.add).then_inc(var1_ready, 1)

            def read_g(i, half=None):
                if isinstance(i, int) and i == 0:
                    dve.wait_ge(c2_ready, 1)
                else:
                    dve.wait_ge(y_made, i * 2)
                dve.wait_ge(rstd1_ready, i + (half or 0) + 1)
                for h in range(2) if half is None else (half,):
                    for n in each(h):
                        ins = nc.vector.scalar_tensor_tensor(out=g_sb[:, n], in0=bank_g[:, n, 0:DOUT],
                                                             scalar=rstd1[:, n:n + 1], in1=c2[:, :],
                                                             op0=ALU.mult, op1=ALU.add)
                    ins.then_inc(g_ready, 1)

            def split_g(i):
                for half in range(2):
                    dve.wait_ge(g_hi_ready, i * 2 + (half + 1))
                    nc.vector.tensor_tensor(g_lo[:, graphs(half)], g_sb[:, graphs(half)],
                                            g_hi[:, graphs(half)].bitcast(F32), ALU.subtract).then_inc(g_lo_ready, 1)

            def split_r(i, k):
                dve.wait_ge(r_hi_ready, i * KH + (k + 1))
                nc.vector.tensor_tensor(r_lo[:, k], r_sb[:, k], r_hi[:, k].bitcast(F32),
                                        ALU.subtract).then_inc(r_lo_ready, 1)

            def add_squares(i, last=False):
                for pair, done in ((0, 2), (1, 4)) if last else ((1, 3), (0, 4)):
                    dve.wait_ge(sq_ready, i * KH + done)
                    nc.vector.tensor_tensor(pair_sb[:, pair], sq_sb[:, 2 * pair], sq_sb[:, 2 * pair + 1],
                                            ALU.add).then_inc(pairs_ready, 1)
                dve.wait_ge(pairs_ready, i * 2 + 2)
                nc.vector.tensor_tensor(q_sb[:, :], pair_sb[:, 0], pair_sb[:, 1], ALU.add).then_inc(q_ready, 1)

            def make_z(i, odd, half):
                if half == 0:
                    if not isinstance(i, int) or i >= 2:
                        dve.wait_ge(stored[odd], (i - odd) * 8)
                    dve.wait_ge(xb_ready, i + 1)
                dve.wait_ge(y_made, i * 2 + (half + 1))
                pair = slice(2 * half, 2 * half + 2)
                nc.vector.scalar_tensor_tensor(out=z_sb[:, odd, pair].rearrange("p n d -> p (n d)"),
                                               in0=xb_sb[:, odd, pair].rearrange("p n d -> p (n d)"),
                                               scalar=2.0, in1=bank_v[:, half], op0=ALU.mult,
                                               op1=ALU.add).then_inc(z_ready, 1)

            def take_stats2(i, odd, half):
                dve.wait_ge(z_ready, i * 2 + (half + 1))
                for n in each(half):
                    ins = nc.vector.bn_stats(bn_sb[:, n], z_sb[:, odd, n])
                ins.then_inc(stats_ready, 1)

            def make_var2(i, half=None):
                part, done = graphs(half), i + (half or 0)
                last = 0 if half is None else 1
                if half is None:
                    dve.wait_ge(out_ready, i)
                dve.wait_ge(stats_ready, i * 2 + (2 if half is None else half + 1))
                if half is None:
                    dve.sem_inc(vector_passed, 1)
                for n in each(half):
                    ins = nc.vector.bn_aggr(mv_sb[:, last, n], bn_sb[:, n])
                ins.then_inc(mean2_ready, 1)
                dve.wait_ge(mean2_ready, done + 1)
                nc.vector.tensor_scalar(mean2[:, last, part], mv_sb[:, last, part, 0], -1.0, None, ALU.mult)
                nc.vector.tensor_scalar(var2[:, last, part], mv_sb[:, last, part, 1], EPS, None,
                                        ALU.add).then_inc(var2_ready, 1)

            make_h(0, 0)
            for n in range(PER):
                ins = nc.vector.scalar_tensor_tensor(out=hw_sb[:, n], in0=adj_sb[:, 0, n], scalar=0.0,
                                                     in1=w_sb[:, 0, n], op0=ALU.not_equal, op1=ALU.mult,
                                                     accum_out=degree[:, 0, n:n + 1])
            ins.then_inc(degree_summed, 1)
            make_d(0)
            dve.wait_ge(d_ready, 1)
            dve.wait_ge(consts_ready, 2)
            for n in range(PER):
                ins = nc.vector.tensor_scalar(diag_sb[:, n], ident[:, :], degree[:, 3, n:n + 1], None, ALU.mult)
            ins.then_inc(diag_ready, 1)
            make_b(0)
            make_at_sb(0, 0)
            dve.wait_ge(w1_hi_ready, 1)
            nc.vector.tensor_tensor(w1_lo[:, :, :], bank_g[:, 0:KD], w1_hi[:, :, :].bitcast(F32),
                                    ALU.subtract).then_inc(w1_ready, 1)
            make_h(1, 1)

            def scale_w2(chunks):
                dve.wait_ge(w2_turned, 1)
                dve.wait_ge(vec_ready, 1)
                for k in chunks:
                    ins = nc.vector.tensor_scalar(w2_g[:, k], bank_g[:, 2 + k // 2, (k % 2) * DOUT:(k % 2 + 1) * DOUT],
                                                  vec[:, KH + k:KH + k + 1], None, ALU.mult)
                ins.then_inc(w2_scaled, 1)

            scale_w2(range(KH // 2))
            split_u(0)
            scale_w2(range(KH // 2, KH))
            dve.wait_ge(w2_scaled, 2)
            nc.vector.tensor_tensor(w2_sum[:, :, :], w2_g[:, 0:2], w2_g[:, 2:4], ALU.add).then_inc(w2_added, 1)
            dve.wait_ge(w2_added, 1)
            nc.vector.tensor_tensor(w2_sum[:, 0], w2_sum[:, 0], w2_sum[:, 1], ALU.add).then_inc(w2_added, 1)
            make_b(1)
            make_d(1)

            def centre_w2():
                dve.wait_ge(w2_summed, 1)
                for k in range(KH):
                    ins = nc.vector.scalar_tensor_tensor(out=w2_g[:, k], in0=bank_g[:, 0, 0:DOUT],
                                                         scalar=-1.0 / HID, in1=w2_g[:, k], op0=ALU.mult, op1=ALU.add)
                ins.then_inc(w2_centred, 1)

            def split_w2():
                dve.wait_ge(w2_hi_ready, 1)
                nc.vector.tensor_tensor(w2_lo[:, :, :], w2_g[:, :, :], w2_hi[:, :, 0:DOUT].bitcast(F32),
                                        ALU.subtract).then_inc(w2_ready, 1)

            def read_c2():
                dve.wait_ge(c2_made, 1)
                nc.vector.tensor_copy(c2[:, :], bank_g[:, 1, 0:DOUT]).then_inc(c2_ready, 1)

            def step(i, odd, first=False, ahead=2):
                if first:
                    centre_w2()
                else:
                    make_var1(i - 1)
                    if ahead:
                        make_b(i + 1)
                    if not isinstance(i, int) or i >= 2:
                        make_var2(i - 2)
                    read_g(i - 1)
                split_r(i, 0)
                if not first:
                    split_g(i - 1)
                if ahead == 2:
                    make_h(i + 2, odd)
                split_r(i, 1)
                if first:
                    split_w2()
                if ahead and not first:
                    make_at_sb(i + 1, 1 - odd)
                split_r(i, 2)
                split_r(i, 3)
                if first:
                    make_at_sb(1, 1)
                    read_c2()
                else:
                    if ahead:
                        make_z(i - 1, 1 - odd, 0)
                        make_z(i - 1, 1 - odd, 1)
                add_squares(i, last=not ahead)
                if ahead:
                    split_u(i + 1, [0])
                else:
                    make_z(i - 1, 1 - odd, 0)
                    make_z(i - 1, 1 - odd, 1)
                if not first:
                    take_stats2(i - 1, 1 - odd, 0)
                if ahead and not first:
                    take_stats2(i - 1, 1 - odd, 1)
                if ahead:
                    split_u(i + 1, [1])
                if ahead == 2:
                    make_d(i + 2)

            pipeline(dve, step)
            def take_last_stats2(half):
                dve.wait_ge(y_made, (GROUPS - 1) * 2 + (half + 1))
                if half == 0:
                    dve.wait_ge(mean2_ready, GROUPS - 1)
                for n in each(half):
                    ins = nc.vector.bn_stats(bn_sb[:, n], last_z[n])
                ins.then_inc(stats_ready, 1)

            make_var1(GROUPS - 1, 0)
            take_stats2(GROUPS - 2, 0, 1)
            make_var2(GROUPS - 2)
            make_var1(GROUPS - 1, 1)
            for half in range(2):
                read_g(GROUPS - 1, half)
            take_last_stats2(0)
            make_var2(GROUPS - 1, 0)
            take_last_stats2(1)
            make_var2(GROUPS - 1, 1)
            dve.wait_ge(stored[1], 8 * (GROUPS - 2))
            for half in range(2):
                dve.wait_ge(rstd2_ready, GROUPS + half)
                for n in each(half):
                    ins = nc.vector.tensor_scalar(z_sb[:, 1, n], last_z[n], mean2[:, 1, n:n + 1],
                                                  rstd2[:, 1, n:n + 1], ALU.add, ALU.mult)
                ins.then_inc(last_out_ready, 1)

        @block.gpsimd
        def _(pool):
            nc.gpsimd.memset(ident[:, :], 0.0).then_inc(consts_zeroed, 1)
            nc.gpsimd.memset(ident_b[:, :], 0.0).then_inc(consts_zeroed, 1)
            for n, m in enumerate((ident, ident_b)):
                pool.wait_ge(consts_zeroed, n + 1)
                nc.gpsimd.affine_select(out=m[:, :], in_=m[:, :], compare_op=ALU.not_equal, fill=1.0, base=0,
                                        pattern=[[-1, P]], channel_multiplier=1).then_inc(consts_ready, 1)
            nc.gpsimd.memset(half_power[:, :], -0.5)
            nc.gpsimd.memset(w2_hi[:, :, DOUT:W2COLS].bitcast(F32), 1.0)
            nc.gpsimd.memset(ones[:, :], 1.0).then_inc(consts_ready, 1)
            pool.wait_ge(consts_ready, 3)
            pool.wait_ge(vec_ready, 1)
            for k in range(KH):
                ins = nc.gpsimd.tensor_scalar(beta_b[:, k], ones[:, :], vec[:, 2 * KH + k:2 * KH + k + 1], 1.0,
                                              ALU.mult, ALU.mult)
            ins.then_inc(beta_ready, 1)
            pool.wait_ge(weights_in[3], 16)
            nc.gpsimd.tensor_scalar(b2_half[:, :], b2_half[:, :], 0.5, 1.0, ALU.mult,
                                    ALU.mult).then_inc(consts_ready, 1)
            nc.gpsimd.tensor_scalar(ident_2[:, :], ident[:, :], 2.0, 1.0, ALU.mult, ALU.mult).then_inc(consts_ready, 1)
            pool.wait_ge(consts_ready, 5)

            def multiply_w(j, odd):
                pool.wait_ge(h_ready, j + 1)
                pool.wait_ge(degree_summed, j)
                nc.gpsimd.tensor_tensor(hw_sb[:, :, :], h_sb[:, :, :], w_sb[:, odd], ALU.mult).then_inc(hw_ready, 1)

            def inverse_std1(i, half=None):
                part = graphs(half)
                pool.wait_ge(var1_ready, i + (half or 0) + 1)
                nc.gpsimd.tensor_tensor(rstd1[:, part], stat1[:, 3, part], half_power[:, part],
                                        ALU.pow).then_inc(rstd1_ready, 1)

            def add_b2(i, odd, y_before):
                pool.wait_ge(x_in[odd], arrival(i, odd, 1))
                if y_before is not None:
                    pool.wait_ge(z_ready, y_before)
                nc.gpsimd.tensor_tensor(xb_sb[:, odd], x_sb[:, odd],
                                        b2_half[:, :].unsqueeze(1).to_broadcast([P, PER, DOUT]),
                                        ALU.add).then_inc(xb_ready, 1)

            def split_r(i, k):
                pool.wait_ge(relu_ready, i * KH + (k + 1))
                pool.sem_inc(pool_passed, 1)
                nc.gpsimd.tensor_scalar(r_hi[:, k], r_sb[:, k], 1.0, 1.0, ALU.mult, ALU.mult).then_inc(r_hi_ready, 1)

            def split_g(i):
                for half in range(2):
                    pool.wait_ge(g_ready, i * 2 + (half + 1))
                    pool.sem_inc(pool_passed, 1)
                    nc.gpsimd.tensor_scalar(g_hi[:, graphs(half)], g_sb[:, graphs(half)], 1.0, 1.0, ALU.mult,
                                            ALU.mult).then_inc(g_hi_ready, 1)

            def split_at(j, odd):
                pool.wait_ge(at_hi_ready, j + 1)
                nc.gpsimd.tensor_tensor(at_lo[:, odd], at_sb[:, :, :], at_hi[:, odd].bitcast(F32),
                                        ALU.subtract).then_inc(at_lo_ready, 1)

            def inverse_std2(i, half=None):
                part, done = graphs(half), i + (half or 0)
                last = 0 if half is None else 1
                pool.wait_ge(var2_ready, done + 1)
                nc.gpsimd.tensor_tensor(rstd2[:, last, part], var2[:, last, part], half_power[:, part],
                                        ALU.pow).then_inc(rstd2_ready, 1)
                if half is not None:
                    return
                pool.wait_ge(rstd2_ready, done + 1)
                nc.gpsimd.tensor_tensor(shift2[:, part], mean2[:, 0, part], rstd2[:, 0, part],
                                        ALU.mult).then_inc(shift2_ready, 1)

            def step(i, odd, first=False, ahead=2):
                if not first:
                    inverse_std1(i - 1)
                split_r(i, 0)
                if not first:
                    split_g(i - 1)
                split_r(i, 1)
                split_r(i, 2)
                split_r(i, 3)
                if not isinstance(i, int) or i >= 2:
                    inverse_std2(i - 2)
                if ahead == 2:
                    multiply_w(i + 2, odd)
                add_b2(i, odd, None if first else i * 2 - 2)
                if ahead:
                    split_at(i + 1, 1 - odd)

            multiply_w(1, 1)
            split_at(0, 0)
            pipeline(pool, step)
            for half in range(2):
                inverse_std1(GROUPS - 1, half)
            inverse_std2(GROUPS - 2)
            for half in range(2):
                inverse_std2(GROUPS - 1, half)


_INS = ["x", "adj", "L0_gnn_W1", "L0_gnn_b1", "L0_gnn_gamma", "L0_gnn_beta", "L0_gnn_W2", "L0_gnn_b2"]


def kernel(**inputs):
    import numpy as _np
    import concourse.bacc as _bacc
    from concourse import mybir as _mybir
    from concourse.bass_utils import run_bass_kernel_spmd as _run

    nc = _bacc.Bacc("TRN2", target_bir_lowering=False, num_devices=1)
    arrays, args = {}, []
    for name in _INS:
        a = _np.ascontiguousarray(inputs[name])
        arrays[f"in_{name}_dram"] = a
        args.append(nc.dram_tensor(f"in_{name}_dram", a.shape, _mybir.dt.from_np(a.dtype), kind="ExternalInput").ap())
    args.append(nc.dram_tensor("out_dram", inputs["x"].shape, _mybir.dt.float32, kind="ExternalOutput").ap())
    hypergraph_block(nc, *args)
    r = _run(nc, [arrays], core_ids=[0])
    return r.results[0]["out_dram"]
```
